# Optimizing a Trainium2 kernel written in Bass

```python
import numpy as np
import jax
import jax.numpy as jnp

def _softmax(x, axis=-1):
    return jax.nn.softmax(x, axis=axis)

def _gelu(x):
    return jax.nn.gelu(x, approximate=True)

def _silu(x):
    return jax.nn.silu(x)

def _sigmoid(x):
    return jax.nn.sigmoid(x)

def _layernorm(x, axis=-1, eps=1e-05):
    m = jnp.mean(x, axis=axis, keepdims=True)
    v = jnp.var(x, axis=axis, keepdims=True)
    return (x - m) / jnp.sqrt(v + eps)

def _scatter_add(tgt, idx, src, axis=0):
    return tgt.at[idx].add(src)

def _segment_sum(src, seg, n):
    return jax.ops.segment_sum(src, seg, n)
kernel_name = 'mk_flamingo_gated_d1_seqx_r8_aa1519'

def setup_inputs(seed: int=0):
    np.random.seed(seed)
    _w = jnp.asarray

    def _rec_inputs():
        import jax
        import jax.numpy as jnp
        _rk = jax.random.key(seed)
        x = 7.22e-05 + 1 * jax.random.normal(jax.random.fold_in(_rk, 1), (32, 64, 512), jnp.float32)
        _lenS = 64 - jax.random.randint(jax.random.fold_in(_rk, 7), (32,), 0, max(1, 64 // 4) + 1, jnp.int32)
        _lenS2 = 64 - jax.random.randint(jax.random.fold_in(_rk, 8), (32,), 0, max(1, 64 // 4) + 1, jnp.int32)
        _ctx_4096P = jax.random.normal(jax.random.fold_in(_rk, 11), (32, 16, 512), jnp.float32)
        _ctx_4096c = jax.random.dirichlet(jax.random.fold_in(_rk, 511), 0.3 * jnp.ones((16,), jnp.float32), (32, 64))
        _ctx_4096t = jnp.einsum('bsk,bkd->bsd', _ctx_4096c, _ctx_4096P)
        _ctx_4096t = _ctx_4096t * jax.lax.rsqrt(jnp.mean(jnp.square(_ctx_4096t)) + 1e-12) * 0.953939
        ctx_4096 = 4.13588e-05 + 0.999923 * (_ctx_4096t + 0.3 * jax.random.normal(jax.random.fold_in(_rk, 611), (32, 64, 512), jnp.float32))
        _g = jax.random.normal(jax.random.fold_in(_rk, 9001), (2, 1), jnp.float32)
        _g = jnp.sign(_g) * jnp.maximum(jnp.abs(_g), 1.0) + (_g == 0) * 1.0
        g_xattn = _g[0]
        g_ffn = _g[1]
        return (x, ctx_4096, g_xattn, g_ffn)
    x, ctx_4096, g_xattn, g_ffn = _rec_inputs()

    def _L0_xattn_setup():
        import jax, jax.numpy as jnp
        import numpy as np
        B, C, N = (4, 64, 512)
        CH = C // 2
        key = jax.random.key(seed)
        ks = jax.random.split(key, 10)
        s = 1.0 / np.sqrt(C)
        return {'Q': jax.random.normal(ks[0], (B, C, N), dtype=jnp.float32), 'K': jax.random.normal(ks[1], (B, C, N), dtype=jnp.float32), 'V': jax.random.normal(ks[2], (B, C, N), dtype=jnp.float32), 'Wq': jax.random.normal(ks[3], (CH, C), dtype=jnp.float32) * s, 'bq': jax.random.normal(ks[4], (CH,), dtype=jnp.float32) * s, 'Wk': jax.random.normal(ks[5], (CH, C), dtype=jnp.float32) * s, 'bk': jax.random.normal(ks[6], (CH,), dtype=jnp.float32) * s, 'Wv': jax.random.normal(ks[7], (C, C), dtype=jnp.float32) * s, 'bv': jax.random.normal(ks[8], (C,), dtype=jnp.float32) * s, 'gamma': jnp.full((1,), 0.5, dtype=jnp.float32)}
    _L0_xattn_all = _L0_xattn_setup()
    _L0_xattn_in = {k: v for k, v in _L0_xattn_all.items() if k in ('Wq', 'bq', 'Wk', 'bk', 'Wv', 'bv', 'gamma')}
    del _L0_xattn_all

    def _L0_ffn_setup():
        import jax, jax.numpy as jnp
        import numpy as np
        DIM = 512
        INTER = 1792
        SPARSITY = 32
        RANK = 16
        key = jax.random.key(seed)
        ks = jax.random.split(key, 5)
        B, T = (32, 1)
        x = jax.random.normal(ks[0], (B, T, DIM), dtype=jnp.float32)
        c1_w = jax.random.normal(ks[1], (RANK, DIM), dtype=jnp.float32) * (1.0 / np.sqrt(DIM))
        c2_w = jax.random.normal(ks[2], (INTER, RANK), dtype=jnp.float32) * (1.0 / np.sqrt(RANK))
        w1 = jax.random.normal(ks[3], (INTER, DIM), dtype=jnp.float32) * (1.0 / np.sqrt(DIM))
        w2t = jax.random.normal(ks[4], (INTER, DIM), dtype=jnp.float32) * (1.0 / np.sqrt(INTER))
        return {'x': x, 'c1_w': c1_w, 'c2_w': c2_w, 'w1': w1, 'w2t': w2t}
    _L0_ffn_all = _L0_ffn_setup()
    _L0_ffn_in = {k: v for k, v in _L0_ffn_all.items() if k in ('c1_w', 'c2_w', 'w1', 'w2t')}
    del _L0_ffn_all
    return {'x': x, 'ctx_4096': ctx_4096, 'g_xattn': g_xattn, 'g_ffn': g_ffn, 'L0_xattn_Wq': _L0_xattn_in['Wq'], 'L0_xattn_bq': _L0_xattn_in['bq'], 'L0_xattn_Wk': _L0_xattn_in['Wk'], 'L0_xattn_bk': _L0_xattn_in['bk'], 'L0_xattn_Wv': _L0_xattn_in['Wv'], 'L0_xattn_bv': _L0_xattn_in['bv'], 'L0_xattn_gamma': _L0_xattn_in['gamma'], 'L0_ffn_c1_w': _L0_ffn_in['c1_w'], 'L0_ffn_c2_w': _L0_ffn_in['c2_w'], 'L0_ffn_w1': _L0_ffn_in['w1'], 'L0_ffn_w2t': _L0_ffn_in['w2t']}

def reference(x, ctx_4096, g_xattn, g_ffn, L0_xattn_Wq, L0_xattn_bq, L0_xattn_Wk, L0_xattn_bk, L0_xattn_Wv, L0_xattn_bv, L0_xattn_gamma, L0_ffn_c1_w, L0_ffn_c2_w, L0_ffn_w1, L0_ffn_w2t):
    import jax
    import jax.numpy as jnp

    def _L0_xattn_ref(Q, K, V, Wq, bq, Wk, bk, Wv, bv, gamma):
        import jax, jax.numpy as jnp
        import numpy as np
        B, C, N = (4, 64, 512)
        CH = C // 2
        q = jnp.einsum('oc,bcn->bon', Wq, Q) + bq[None, :, None]
        k = jnp.einsum('oc,bcn->bon', Wk, K) + bk[None, :, None]
        v = jnp.einsum('oc,bcn->bon', Wv, V) + bv[None, :, None]
        energy = jnp.einsum('bcn,bcm->bnm', q, k)
        attention = jax.nn.softmax(energy, axis=-1)
        out = jnp.einsum('bcm,bnm->bcn', v, attention)
        return gamma * out + V

    def _L0_ffn_ref(x, c1_w, c2_w, w1, w2t):
        import jax, jax.numpy as jnp
        import numpy as np
        DIM = 512
        INTER = 1792
        SPARSITY = 32
        RANK = 16
        B, T, M = x.shape
        xf = x.reshape(B * T, M)
        inter = xf @ c1_w.T @ c2_w.T
        n_blocks = INTER // SPARSITY
        blk = inter.reshape(B * T, n_blocks, SPARSITY)
        idx = jnp.argmax(blk, axis=-1) + jnp.arange(0, INTER, SPARSITY)
        w1_g = w1[idx]
        w2_g = w2t[idx]
        h = jax.nn.relu(jnp.einsum('bkm,bm->bk', w1_g, xf))
        out = jnp.einsum('bk,bkm->bm', h, w2_g)
        return out.reshape(B, T, M)
    x = x + jnp.tanh(g_xattn[0]) * _L0_xattn_ref(_layernorm(x, axis=-1), ctx_4096, ctx_4096, L0_xattn_Wq, L0_xattn_bq, L0_xattn_Wk, L0_xattn_bk, L0_xattn_Wv, L0_xattn_bv, L0_xattn_gamma)
    x = x + jnp.tanh(g_ffn[0]) * _L0_ffn_ref(_layernorm(x, axis=-1), L0_ffn_c1_w, L0_ffn_c2_w, L0_ffn_w1, L0_ffn_w2t)
    return x

_drawn_inputs = setup_inputs


def setup_inputs(seed=0):
    import zlib

    import numpy as np

    out = dict(_drawn_inputs(seed))
    spreads = {}
    factors = {}
    for name, (base, spread) in spreads.items():
        noise = np.random.default_rng([zlib.crc32(name.encode()), seed]).standard_normal(out[name].shape)
        drawn = base * np.exp(spread * noise) if base else spread * noise
        out[name] = jnp.asarray(drawn.astype(out[name].dtype))
    for name, factor in factors.items():
        out[name] = (out[name] * factor).astype(out[name].dtype)
    return out
```

```python
from contextlib import ExitStack

import concourse.bass as bass
from concourse import mybir

F32 = mybir.dt.float32
F32R = mybir.dt.float32r
F16 = mybir.dt.float16
BF16 = mybir.dt.bfloat16
F8 = mybir.dt.float8e4
I32 = mybir.dt.int32
ALU = mybir.AluOpType
ACT = mybir.ActivationFunctionType
AX_X = mybir.AxisListType.X
RMAX = bass.bass_isa.ReduceOp.max

P = 128
B, C, N = 32, 64, 512
CH = C // 2
INTER, BLK, RANK = 1792, 32, 16
PAIRS = B // 2
TP = 4
TILES = PAIRS // TP
TOK = TP * P
NU = INTER // P
NC = N // P
MC = 4
MW = INTER // MC
EPS = 1e-5
SH_ROW = 96
BIG = 16384.0
W1_EXP = 3
W2_EXP = 10
RING = 3
USES = 24


def pair_items():
    return [("proj", 0, 0), ("proj", 0, 1), ("residual", -1, 0), ("ctx_t", 0, 0), ("energy", 0, 0), ("x2_t", -1, 0),
            ("energy", 0, 1), ("rank", -1, 0), ("shift", 0, 0), ("mask", -1, 0), ("handoff", 0, 0),
            ("probs", 0, 0), ("shift", 0, 1), ("weigh", 0, 0), ("prep", 1, 0), ("probs", 0, 1), ("weigh", 0, 1),
            ("attn_out", 0, 0)]


def spread(items, fillers):
    out, done = [], 0
    for n, item in enumerate(items):
        out.append(item)
        upto = len(fillers) * (n + 1) // len(items)
        out += fillers[done:upto]
        done = upto
    return out


def ffn_pieces():
    return [("units", u) for u in range(NU)] + [("down", j, h) for j in range(TP) for h in range(2)]


def weight_pieces():
    return [("w1", u) for u in range(NU)] + [("w2_max", u) for u in range(NU)] + [("w2_scale", 0)] + \
        [("w2", u) for u in range(NU)]


def plan_first():
    items = [("setup", 0, 0), ("prep", 0, 0)]
    for j in range(TP):
        for name, d, b in pair_items():
            if name == "handoff" or (j == 0 and d < 0):
                continue
            items.append((name, j + d, b))
    return spread(items, weight_pieces())


def plan_loop(final=False):
    items = []
    for j in range(TP):
        for name, d, b in pair_items():
            if name == "handoff" and j > 0 or name == "prep" and final and j == TP - 1:
                continue
            items.append((name, TP + j + d, b))
    at = items.index(("handoff", TP, 0)) + 1
    return items[:at] + spread(items[at:], ffn_pieces())


def plan_last():
    items = [(name, TP + d, b) for name, d, b in pair_items() if d < 0]
    return items + [("handoff", TP, 0)] + ffn_pieces()


def build(nc, x, ctx, w1, w2, wq, wk, wv, bq, bk, bv, c1, c2, scal, ident, tie, out):
    with ExitStack() as es:
        def sb(name, shape, dt):
            return es.enter_context(nc.sbuf_tensor(name, shape, dt))

        def sem(name):
            return es.enter_context(nc.semaphore(name))

        w1h, w1l = sb("w1h", [P, NC, INTER], F16), sb("w1l", [P, NC, INTER], F16)
        w2h, w2l = sb("w2h", [P, NU, N], F16), sb("w2l", [P, NU, N], F16)
        c1h, c1l = sb("c1h", [P, NC, P], F16), sb("c1l", [P, NC, P], F16)
        c2s = sb("c2s", [P, INTER], F32R)
        wqh, wql = sb("wqh", [P, P], F32R), sb("wql", [P, P], F32R)
        wkh, wkl = sb("wkh", [P, P], F32R), sb("wkl", [P, P], F32R)
        wvh, wvl = sb("wvh", [P, 2, P], F32R), sb("wvl", [P, 2, P], F32R)
        bqc, bkc, bvc = sb("bqc", [P, 1], F32), sb("bkc", [P, 1], F32), sb("bvc", [P, 1], F32)
        sc = sb("sc", [P, 3], F32)
        tanhs = sb("tanhs", [P, 2], F32)
        gbv = sb("gbv", [P, 1], F32)
        ffn_scale = sb("ffn_scale", [P, 1], F32)
        idf = sb("idf", [P, P], F32)
        idb = sb("idb", [P, P], BF16)
        tieb = sb("tieb", [P, P], BF16)
        neg_row, one_row = sb("neg_row", [1, P], BF16), sb("one_row", [1, TOK], BF16)
        half = sb("half", [P, 1], F32)
        rmax, rexp = sb("rmax", [P, NU + 1], F32), sb("rexp", [P, NU + 1], I32)
        rscale, rinv = sb("rscale", [P, NU + 1], I32), sb("rinv", [P, NU + 1], I32)
        w2max, w2q = sb("w2max", [P, NU], F32), sb("w2q", [P, NU], F32)
        gmax = sb("gmax", [P, 2], F32)
        gexp = sb("gexp", [P, 3], I32)
        w2scale = sb("w2scale", [P, NU], F32)
        xt, ct = sb("xt", [P, 2, N], F32), sb("ct", [P, 2, N], F32)
        xn = sb("xn", [P, N], F32)
        xh, xl = sb("xh", [P, N], F32R), sb("xl", [P, N], F32R)
        ch, cl = sb("ch", [P, N], F32R), sb("cl", [P, N], F32R)
        stat, mv, rstd = sb("stat", [P, 2, 6], F32), sb("mv", [P, 2, 2], F32), sb("rstd", [P, 2, 2], F32)
        qs, ks = sb("qs", [P, 2, N], F32R), sb("ks", [P, 2, N], F32R)
        vt = sb("vt", [P, 2, NC, P], F32R)
        nmax, ssum = sb("nmax", [P, 2, NC], F32), sb("ssum", [P, 2, NC], F32)
        lns, shf = sb("lns", [P, 2, NC], F32), sb("shf", [P, 2, NC], F32)
        shm = sb("shm", [P, NC, P], F32)
        ph, pl = sb("ph", [P, NC, N], F32R), sb("pl", [P, NC, N], F32R)
        pf = sb("pf", [P, 2, N], F32)
        uh, ul = sb("uh", [P, 2, N], F32R), sb("ul", [P, 2, N], F32R)
        att = sb("att", [P, N], F32)
        y = sb("y", [P, N], F32)
        ts = sb("ts", [P, P], F32R)
        bmax = sb("bmax", [P, 2, MW // BLK], F32)
        x2hn, x2ln = sb("x2hn", [P, NC, TOK], F16), sb("x2ln", [P, NC, TOK], F16)
        x2hc, x2lc = sb("x2hc", [P, NC, TOK], F16), sb("x2lc", [P, NC, TOK], F16)
        eqn, eqc = sb("eqn", [P, TP, INTER], F8), sb("eqc", [P, TP, INTER], F8)
        resn, resc = sb("resn", [P, TP, N], F32), sb("resc", [P, TP, N], F32)
        eqt = sb("eqt", [P, 2, TOK], BF16)
        hh, hl = sb("hh", [P, NU, TOK], F16), sb("hl", [P, NU, TOK], F16)

        ring = [es.enter_context(nc.psum_tensor(f"ring{i}", [P, N], F32)) for i in range(RING)]
        psU = es.enter_context(nc.psum_tensor("psU", [P, N], F32))
        psF = [es.enter_context(nc.psum_tensor(f"psF{i}", [P, N], F32)) for i in range(2)]
        psE = es.enter_context(nc.psum_tensor("psE", [P, N], F32))
        psM = es.enter_context(nc.psum_tensor("psM", [P, N], F32))

        s_small, s_x, s_w, s_out = sem("s_small"), [sem("s_x0"), sem("s_x1")], [sem(f"s_w{i}") for i in range(4)], sem("s_out")
        s_const, s_cast, s_tanh, s_c1pre, s_c1ps, s_c1hi, s_setup = (
            sem(n) for n in ("const", "cast", "tanh", "c1pre", "c1ps", "c1hi", "setup"))
        s_rs, s_wsc, s_wps, s_whi, s_wlo, s_free, s_gc, s_gall, s_w2hi, s_w2lo = (
            sem(n) for n in ("rs", "wsc", "wps", "whi", "wlo", "wfree", "gchain", "gall", "w2hi", "w2lo"))
        s_bn, s_pow, s_xn, s_hic, s_loc = (sem(n) for n in ("bn", "pow", "xn", "hic", "loc"))
        s_qkps, s_qkhi, s_qk = sem("qkps"), sem("qkhi"), sem("qk")
        s_ctps, s_cthi, s_vt = sem("ctps"), sem("cthi"), sem("vt")
        s_eps, s_emax, s_eexp = sem("eps"), sem("emax"), sem("eexp")
        s_ln, s_shc, s_shps, s_shin = sem("ln"), sem("shc"), sem("shps"), sem("shin")
        s_tps, s_thi, s_texp, s_pl, s_pv = sem("tps"), sem("thi"), sem("texp"), sem("pl"), sem("pv")
        s_uhi, s_u, s_ops, s_att, s_res = sem("uhi"), sem("u"), sem("ops"), sem("att"), sem("res")
        s_x2ps, s_x2hi, s_x2, s_rps, s_rhi, s_rank = (sem(n) for n in ("x2ps", "x2hi", "x2", "rps", "rhi", "rank"))
        s_mps, s_bmax, s_eq, s_hand = sem("mps"), sem("bmax"), sem("eq"), sem("hand")
        s_eqps, s_eqt, s_hps, s_hhi, s_h, s_dps, s_done = (
            sem(n) for n in ("eqps", "eqt", "hps", "hhi", "h", "dps", "done"))

        s_passed = {nc.vector.engine: sem("passed_dve"), nc.tensor.engine: sem("passed_pe")}
        s_x2pow, s_rsum, s_rsn, s_x2n = sem("x2pow"), sem("rsum"), sem("rsn"), sem("x2n")
        hraw = hh.ap().rearrange("p u k -> p (u k)")[:, 0:2 * (5 * P + N)].bitcast(F32)
        NSMALL, NCAST = 11, 12

        block = es.enter_context(nc.Block())

        def wait(eng, s, value):
            if not isinstance(value, int) or value > 0:
                eng.wait_ge(s, value)

        def carry_wait(eng):
            eng.sem_inc(s_passed[eng.engine], 1)

        def walk(eng, steps):
            def go(plan, p0, t):
                for name, k, *rest in plan:
                    if name not in steps:
                        continue
                    if name in ("units", "down"):
                        steps[name](t, k, *rest)
                    elif name in ("w1", "w2_max", "w2_scale", "w2", "setup"):
                        steps[name](k)
                    elif name == "handoff":
                        steps[name](t)
                    else:
                        steps[name](p0 + k, k % TP, *rest)
            go(plan_first(), 0, 0)
            with eng.Fori(0, TILES - 2) as t:
                go(plan_loop(), TP * t, t)
            go(plan_loop(final=True), TP * (TILES - 2), TILES - 2)
            go(plan_last(), TP * (TILES - 1), TILES - 1)

        FREE = [(s_qk, 4, 1), (s_qk, 4, 2), (s_qk, 4, 3), (s_qk, 4, 4), (s_vt, 1, 1)]
        FREE += [(s_eexp, 8, n + 1) for n in range(8)] + [(s_shin, 2, 1)]
        FREE += [(s_texp, 8, n + 1) for n in range(4)] + [(s_shin, 2, 2)]
        FREE += [(s_texp, 8, n + 1) for n in range(4, 8)] + [(s_att, 1, 1)]
        Q0, CT0, E0, S0, T0, S1, T1, O0 = 0, 4, 5, 13, 14, 18, 19, 23

        @block.sync
        def _(eng):
            def load_pair(p, slot):
                eng.dma_start(xt[:, slot, :], x[p]).then_inc(s_x[slot], 16)
                eng.dma_start(ct[:, slot, :], ctx[p]).then_inc(s_x[slot], 16)

            wloads = [(w1, u) for u in range(NU)] + [(w2, u) for u in range(NU)] * 2

            def load_weights(n):
                if n < len(wloads):
                    src, u = wloads[n]
                    if n < 4:
                        eng.wait_ge(s_setup, 1)
                    else:
                        eng.wait_ge(s_free, n - 3)
                    eng.dma_start(resc[:, n % 4, :], src[u]).then_inc(s_w[n % 4], 16)

            def setup(_):
                load_pair(0, 0)
                eng.dma_start(hraw[:, 0:P], wq).then_inc(s_small, 16)
                eng.dma_start(hraw[:, P:2 * P], wk).then_inc(s_small, 16)
                eng.dma_start(hraw[:, 2 * P:4 * P], wv).then_inc(s_small, 16)
                eng.dma_start(hraw[:, 4 * P:5 * P], tie).then_inc(s_small, 16)
                eng.dma_start(idf[:, :], ident).then_inc(s_small, 16)
                eng.dma_start(bqc[:, :], bq).then_inc(s_small, 16)
                eng.dma_start(bkc[:, :], bk).then_inc(s_small, 16)
                eng.dma_start(bvc[:, :], bv).then_inc(s_small, 16)
                eng.dma_start(sc[:, :], scal).then_inc(s_small, 16)
                eng.dma_start(hraw[:, 5 * P:5 * P + N], c1).then_inc(s_small, 16)
                eng.dma_start(resc.ap().rearrange("p a b -> p (a b)")[:, 0:INTER], c2).then_inc(s_small, 16)
                load_pair(1, 1)
                for n in range(3):
                    load_weights(n)

            def residual(p, j, b):
                eng.wait_ge(s_rsn, p + 1)
                load_pair(p + 2, j % 2)

            def w_piece(kind):
                base = {"w1": 0, "w2_max": NU, "w2": 2 * NU}[kind]
                return lambda u: load_weights(base + u + 3)

            def down(t, j, h):
                if h == 1:
                    eng.wait_ge(s_done, TP * t + j + 1)
                    eng.dma_start(out[TP * t + j], resc[:, j, :]).then_inc(s_out, 16)

            steps = {"setup": setup, "residual": residual, "w1": w_piece("w1"), "w2_max": w_piece("w2_max"),
                     "w2": w_piece("w2"), "down": down}

            def go(plan, p0, t, last_pair):
                for name, k, *rest in plan:
                    if name == "residual":
                        if last_pair is None or k + 2 <= last_pair:
                            residual(p0 + k, k % TP, 0)
                    elif name == "down":
                        down(t, k, *rest)
                    elif name in steps:
                        steps[name](k)
            go(plan_first(), 0, 0, None)
            with eng.Fori(0, TILES - 2) as t:
                go(plan_loop(), TP * t, t, None)
            go(plan_loop(), TP * (TILES - 2), TILES - 2, 2 * TP - 1)
            go([s for s in plan_last() if s[0] != "residual"], TP * (TILES - 1), TILES - 1, None)
            eng.wait_ge(s_out, 16 * PAIRS)

        @block.gpsimd
        def _(eng):
            eng.memset(half[:, :], -0.5).then_inc(s_const, 1)
            eng.memset(neg_row[:, :], -BIG).then_inc(s_const, 1)
            eng.memset(one_row[:, :], 1.0).then_inc(s_const, 1)
            eng.memset(shm[:, :, :], 0.0).then_inc(s_const, 1)
            eng.wait_ge(s_const, 4)

            def prep(p, j, b):
                eng.wait_ge(s_bn, 3 * (p + 1))
                wait(eng, s_xn, 2 * p)
                eng.tensor_tensor(rstd[:, 0, 1:2], rstd[:, 0, 0:1], half[:, :], ALU.pow).then_inc(s_pow, 1)
                eng.wait_ge(s_hic, p + 1)
                wait(eng, s_qkps, 4 * p)
                eng.tensor_tensor(cl[:, :], ct[:, j % 2, :], ch[:, :].bitcast(F32), ALU.subtract).then_inc(s_loc, 1)
                eng.wait_ge(s_xn, 2 * p + 2)
                eng.tensor_tensor(xl[:, :], xn[:, :], xh[:, :].bitcast(F32), ALU.subtract).then_inc(s_loc, 1)

            def x2_t(p, j, b):
                eng.wait_ge(s_res, 3 * (p + 1))
                eng.tensor_tensor(rstd[:, 1, 1:2], rstd[:, 1, 0:1], half[:, :], ALU.pow).then_inc(s_x2pow, 1)

            def w2_scale(_):
                eng.wait_ge(s_gc, 2)
                eng.partition_all_reduce(gmax[:, 1:2], gmax[:, 0:1], P, RMAX).then_inc(s_gall, 1)

            def w2_low(u):
                n = 2 * NU + u
                eng.wait_ge(s_w2hi, 2 * (u + 1))
                eng.tensor_tensor(w2l[:, u, :], resc[:, n % 4, :], w2h[:, u, :], ALU.subtract).then_inc(s_free, 1)

            walk(eng, {"prep": prep, "x2_t": x2_t, "w2_scale": w2_scale, "w2": w2_low})

        @block.scalar
        def _(eng):
            act = eng.activation

            def setup(_):
                eng.wait_ge(s_small, 16 * NSMALL)
                act(tanhs[:, :], sc[:, 0:2], ACT.Tanh).then_inc(s_tanh, 1)
                eng.wait_ge(s_c1ps, 1)
                act(c1h[:, :, :], psE[:, :].rearrange("p (c r) -> p c r", c=NC), ACT.Copy).then_inc(s_c1hi, 1)
                eng.wait_ge(s_cast, NCAST)

            def proj(p, j, b):
                for i, (dst, bias) in enumerate(((qs, bqc), (ks, bkc))):
                    n = 2 * b + i
                    eng.wait_ge(s_qkps, 4 * p + n + 1)
                    wait(eng, s_tps, 8 * p - 4 + 4 * b)
                    act(dst[:, b, :], ring[(Q0 + n) % RING][:, :], ACT.Identity, bias=bias[:, 0:1]).then_inc(s_qkhi, 1)

            def ctx_t(p, j, b):
                eng.wait_ge(s_ctps, p + 1)
                wait(eng, s_pv, 8 * p)
                act(vt[:, :, :, 0:C], ring[CT0 % RING][:, :].rearrange("p (t b c) -> p b t c", t=NC, b=2),
                    ACT.Copy).then_inc(s_cthi, 1)

            def energy(p, j, b):
                for i in range(NC):
                    n = 4 * b + i
                    eng.wait_ge(s_emax, 8 * p + n + 1)
                    if i == 0:
                        wait(eng, s_ln, 2 * p - 1 + b)
                    bank = ring[(E0 + n) % RING]
                    act(bank[:, :], bank[:, :], ACT.Exp, bias=nmax[:, b, i:i + 1],
                        accum_out=ssum[:, b, i:i + 1]).then_inc(s_eexp, 1)

            def shift(p, j, b):
                eng.wait_ge(s_eexp, 8 * p + 4 * b + 4)
                wait(eng, s_shc, 6 * p - 3 + 3 * b)
                act(lns[:, b, :], ssum[:, b, :], ACT.Ln).then_inc(s_ln, 1)
                eng.wait_ge(s_shps, 2 * p + b + 1)
                bank = ring[(S0, S1)[b] % RING]
                act(qs[SH_ROW:P, b, :], bank[SH_ROW:P, :], ACT.Copy).then_inc(s_shin, 1)

            def probs(p, j, b):
                for i in range(NC):
                    n = 4 * b + i
                    bank = ring[((T0, T1)[b] + i) % RING]
                    eng.wait_ge(s_tps, 8 * p + n + 1)
                    wait(eng, s_pv, 8 * p + n - 3)
                    act(ph[:, i, :], bank[:, :], ACT.Exp).then_inc(s_thi, 1)
                    wait(eng, s_pl, 8 * p + n - 1)
                    act(pf[:, n % 2, :], bank[:, :], ACT.Exp).then_inc(s_texp, 1)

            def weigh(p, j, b):
                eng.wait_ge(s_pv, 8 * p + 4 * b + 4)
                wait(eng, s_ops, p)
                act(uh[:, b, :], psU[:, :], ACT.Copy).then_inc(s_uhi, 1)

            def attn_out(p, j, b):
                eng.wait_ge(s_ops, p + 1)
                wait(eng, s_rsn, p)
                act(att[:, :], ring[O0 % RING][:, :], ACT.Identity, bias=gbv[:, 0:1], scale=sc[:, 2:3]).then_inc(s_att, 1)

            def x2_t(p, j, b):
                eng.wait_ge(s_x2ps, p + 1)
                if not isinstance(p, int) or p >= TP:
                    eng.wait_ge(s_hand, 4 * (p // TP) if isinstance(p, int) else hand_of(p, j))
                act(x2hn[:, :, j * P:(j + 1) * P], psM[:, :].rearrange("p (c k) -> p c k", c=NC), ACT.Copy).then_inc(s_x2hi, 1)

            def hand_of(p, j):
                return p - j

            def w1_high(u):
                eng.wait_ge(s_wps, u + 1)
                act(w1h[:, :, u * P:(u + 1) * P], psF[u % 2][:, :].rearrange("p (c k) -> p c k", c=NC),
                    ACT.Copy).then_inc(s_whi, 1)

            def units(t, u):
                n = NU * t + u
                eng.wait_ge(s_eqps, n + 1)
                wait(eng, s_hps, NU * t + max(u - 1, 0))
                act(eqt[:, u % 2, :], psE[:, :], ACT.Copy).then_inc(s_eqt, 1)
                eng.wait_ge(s_hps, n + 1)
                if u == 0:
                    wait(eng, s_dps, TP * t)
                act(hh[:, u, :], psF[u % 2][:, :], ACT.Relu).then_inc(s_hhi, 1)

            walk(eng, {"setup": setup, "proj": proj, "ctx_t": ctx_t, "energy": energy, "shift": shift, "probs": probs,
                       "weigh": weigh, "attn_out": attn_out, "x2_t": x2_t, "w1": w1_high, "units": units})

        @block.vector
        def _(eng):
            def low(dst, full, high):
                return eng.tensor_tensor(dst, full, high, ALU.subtract)

            def scale_of(col, src, chain):
                eng.tensor_reduce(rmax[:, col:col + 1], src, AX_X, ALU.max, apply_absolute_value=True).then_inc(s_rs, 1)
                eng.wait_ge(s_rs, chain + 1)
                eng.tensor_scalar(rmax[:, col:col + 1], rmax[:, col:col + 1], 1e-30, None, ALU.max).then_inc(s_rs, 1)
                eng.wait_ge(s_rs, chain + 2)
                eng.tensor_scalar(rexp[:, col:col + 1], rmax[:, col:col + 1].bitcast(I32), 0x7F800000, None,
                                  ALU.bitwise_and).then_inc(s_rs, 1)
                eng.wait_ge(s_rs, chain + 3)
                eng.tensor_scalar(rscale[:, col:col + 1], rexp[:, col:col + 1], -1.0, float((254 + W1_EXP) << 23),
                                  ALU.mult, ALU.add).then_inc(s_rs, 1)
                eng.tensor_scalar(rinv[:, col:col + 1], rexp[:, col:col + 1], float(-(W1_EXP << 23)), None,
                                  ALU.add).then_inc(s_rs, 1)
                eng.wait_ge(s_rs, chain + 5)

            def setup(_):
                eng.wait_ge(s_small, 16 * NSMALL)
                cast = [(wqh[:, :], hraw[:, 0:P]), (wkh[:, :], hraw[:, P:2 * P]),
                        (wvh.ap().rearrange("p b k -> p (b k)"), hraw[:, 2 * P:4 * P]),
                        (tieb[:, :], hraw[:, 4 * P:5 * P]), (idb[:, :], idf[:, :]),
                        (c2s[:, :], resc.ap().rearrange("p a b -> p (a b)")[:, 0:INTER])]
                for dst, src in cast:
                    eng.tensor_copy(dst, src).then_inc(s_cast, 1)
                eng.wait_ge(s_cast, len(cast))
                low(wql[:, :], hraw[:, 0:P], wqh[:, :].bitcast(F32)).then_inc(s_cast, 1)
                low(wkl[:, :], hraw[:, P:2 * P], wkh[:, :].bitcast(F32)).then_inc(s_cast, 1)
                low(wvl.ap().rearrange("p b k -> p (b k)"), hraw[:, 2 * P:4 * P],
                    wvh.ap().rearrange("p b k -> p (b k)").bitcast(F32)).then_inc(s_cast, 1)
                eng.tensor_tensor(gbv[:, :], bvc[:, :], sc[:, 2:3], ALU.mult).then_inc(s_cast, 1)
                for r in (32, 96):
                    rows = slice(r, r + 32)
                    ins = low(c2s[rows, :], resc.ap().rearrange("p a b -> p (a b)")[rows, 0:INTER],
                              c2s[rows, :].bitcast(F32))
                    ins.then_inc(s_cast if r == 32 else s_setup, 1)
                raw = hraw[:, 5 * P:5 * P + N]
                scale_of(NU, raw, 0)
                eng.tensor_scalar(raw, raw, rscale[:, NU:NU + 1].bitcast(F32), None, ALU.mult).then_inc(s_c1pre, 1)
                eng.wait_ge(s_c1hi, 1)
                low(c1l[:, :, :], psE[:, :].rearrange("p (c r) -> p c r", c=NC), c1h[:, :, :]).then_inc(s_cast, 1)

            def prep(p, j, b):
                k = j % 2
                eng.wait_ge(s_x[k], 32 * (p // 2 + 1) if isinstance(p, int) else 16 * (p - k) + 32)
                eng.bn_stats(stat[:, 0, :], xt[:, k, :]).then_inc(s_bn, 1)
                wait(eng, s_qkps, 4 * p)
                wait(eng, s_loc, 2 * p)
                eng.tensor_copy(ch[:, :], ct[:, k, :]).then_inc(s_hic, 1)
                wait(eng, s_xn, 2 * p)
                eng.wait_ge(s_bn, 3 * p + 1)
                carry_wait(eng)
                eng.bn_aggr(mv[:, 0, :], stat[:, 0, :]).then_inc(s_bn, 1)
                eng.wait_ge(s_bn, 3 * p + 2)
                wait(eng, s_pow, p)
                eng.tensor_scalar(rstd[:, 0, 0:1], mv[:, 0, 1:2], EPS, None, ALU.add).then_inc(s_bn, 1)
                eng.wait_ge(s_pow, p + 1)
                eng.tensor_scalar(xn[:, :], xt[:, k, :], mv[:, 0, 0:1], rstd[:, 0, 1:2], ALU.subtract, ALU.mult).then_inc(s_xn, 1)
                eng.tensor_scalar(xh[:, :], xt[:, k, :], mv[:, 0, 0:1], rstd[:, 0, 1:2], ALU.subtract, ALU.mult).then_inc(s_xn, 1)

            def proj(p, j, b):
                for i, (dst, bias, row) in enumerate(((qs, bqc, 64), (ks, bkc, 32))):
                    n = 2 * b + i
                    rows = slice(row, row + 32)
                    eng.wait_ge(s_qkhi, 4 * p + n + 1)
                    eng.scalar_tensor_tensor(out=dst[rows, b, :], in0=ring[(Q0 + n) % RING][rows, :], scalar=bias[rows, 0:1],
                                             in1=dst[rows, b, :].bitcast(F32), op0=ALU.add, op1=ALU.subtract).then_inc(s_qk, 1)

            def ctx_t(p, j, b):
                eng.wait_ge(s_cthi, p + 1)
                wait(eng, s_pv, 8 * p)
                low(vt[:, :, :, C:P], ring[CT0 % RING][:, :].rearrange("p (t b c) -> p b t c", t=NC, b=2),
                    vt[:, :, :, 0:C].bitcast(F32)).then_inc(s_vt, 1)

            def energy(p, j, b):
                if True:
                    wait(eng, s_shc, 6 * p - 3 + 3 * b)
                for i in range(NC):
                    n = 4 * b + i
                    eng.wait_ge(s_eps, 8 * p + n + 1)
                    eng.tensor_reduce(nmax[:, b, i:i + 1], ring[(E0 + n) % RING][:, :], AX_X, ALU.max,
                                      negate=True).then_inc(s_emax, 1)

            def shift(p, j, b):
                eng.wait_ge(s_ln, 2 * p + b + 1)
                eng.wait_ge(s_emax, 8 * p + 4 * b + 4)
                wait(eng, s_shps, 2 * p + b)
                c = 6 * p + 3 * b
                eng.tensor_tensor(shm[:, :, SH_ROW].bitcast(F32R), nmax[:, b, :], lns[:, b, :], ALU.subtract).then_inc(s_shc, 1)
                eng.tensor_tensor(shf[:, b, :], nmax[:, b, :], lns[:, b, :], ALU.subtract).then_inc(s_shc, 1)
                eng.wait_ge(s_shc, c + 2)
                low(shm[:, :, SH_ROW + 1], shf[:, b, :], shm[:, :, SH_ROW]).then_inc(s_shc, 1)

            def probs(p, j, b):
                for i in range(NC):
                    n = 4 * b + i
                    eng.wait_ge(s_texp, 8 * p + n + 1)
                    wait(eng, s_pv, 8 * p + n - 3)
                    low(pl[:, i, :], pf[:, n % 2, :], ph[:, i, :].bitcast(F32)).then_inc(s_pl, 1)

            def weigh(p, j, b):
                eng.wait_ge(s_uhi, 2 * p + b + 1)
                wait(eng, s_ops, p)
                low(ul[:, b, :], psU[:, :], uh[:, b, :].bitcast(F32)).then_inc(s_u, 1)

            def residual(p, j, b):
                k = j % 2
                eng.wait_ge(s_att, p + 1)
                if not isinstance(p, int) or p >= TP:
                    eng.wait_ge(s_hand, p - j)
                wait(eng, s_x2n, 2 * p)
                eng.tensor_tensor(att[:, :], att[:, :], ct[:, k, :], ALU.add).then_inc(s_rsum, 1)
                eng.wait_ge(s_rsum, p + 1)
                eng.scalar_tensor_tensor(out=resn[:, j, :], in0=att[:, :], scalar=tanhs[:, 0:1], in1=xt[:, k, :],
                                         op0=ALU.mult, op1=ALU.add).then_inc(s_rsn, 1)
                eng.wait_ge(s_rsn, p + 1)
                eng.bn_stats(stat[:, 1, :], resn[:, j, :]).then_inc(s_res, 1)
                eng.wait_ge(s_res, 3 * p + 1)
                carry_wait(eng)
                eng.bn_aggr(mv[:, 1, :], stat[:, 1, :]).then_inc(s_res, 1)
                eng.wait_ge(s_res, 3 * p + 2)
                wait(eng, s_x2pow, p)
                eng.tensor_scalar(rstd[:, 1, 0:1], mv[:, 1, 1:2], EPS, None, ALU.add).then_inc(s_res, 1)

            def norm(p, j):
                eng.wait_ge(s_x2pow, p + 1)
                wait(eng, s_x2ps, p)
                eng.tensor_scalar(y[:, :], resn[:, j, :], mv[:, 1, 0:1], rstd[:, 1, 1:2], ALU.subtract,
                                  ALU.mult).then_inc(s_x2n, 2)

            def x2_t(p, j, b):
                norm(p, j)
                eng.wait_ge(s_x2hi, p + 1)
                cols = slice(j * P, (j + 1) * P)
                low(x2ln[:, :, cols], psM[:, :].rearrange("p (c k) -> p c k", c=NC), x2hn[:, :, cols]).then_inc(s_x2, 1)

            def rank(p, j, b):
                eng.wait_ge(s_rps, p + 1)
                wait(eng, s_mps, MC * p)
                inv = rinv[:, NU:NU + 1].bitcast(F32)
                eng.tensor_scalar(ts[:, :], psM[:, 0:P], inv, None, ALU.mult).then_inc(s_rhi, 1)
                eng.wait_ge(s_rhi, p + 1)
                rows = slice(64, P)
                eng.scalar_tensor_tensor(out=ts[rows, :], in0=psM[rows, 0:P], scalar=inv[rows, :], in1=ts[rows, :].bitcast(F32),
                                         op0=ALU.mult, op1=ALU.subtract).then_inc(s_rank, 1)

            def mask(p, j, b):
                for c in range(MC):
                    v = psM[:, 0:MW].rearrange("p (n k) -> p n k", k=BLK)
                    n = MC * p + c
                    eng.wait_ge(s_mps, n + 1)
                    wait(eng, s_eq, n - 1)
                    bm = bmax[:, c % 2, :]
                    eng.tensor_reduce(bm, v, AX_X, ALU.max).then_inc(s_bmax, 1)
                    eng.wait_ge(s_bmax, n + 1)
                    carry_wait(eng)
                    eng.tensor_tensor(eqn[:, j, c * MW:(c + 1) * MW].rearrange("p (n k) -> p n k", k=BLK), v,
                                      bm.unsqueeze(2).broadcast_to([P, MW // BLK, BLK]), ALU.is_equal,
                                      saturate=False).then_inc(s_eq, 1)

            def handoff(t):
                eng.wait_ge(s_x2, TP * (t + 1))
                eng.wait_ge(s_eq, MC * TP * (t + 1))
                eng.wait_ge(s_x2hi, TP * (t + 1))
                wait(eng, s_hps, NU * t)
                if isinstance(t, int) and t == 0:
                    pass
                eng.tensor_copy(x2hc[:, :, :], x2hn[:, :, :]).then_inc(s_hand, 1)
                eng.tensor_copy(x2lc[:, :, :], x2ln[:, :, :]).then_inc(s_hand, 1)
                eng.tensor_copy(eqc[:, :, :].bitcast(I32), eqn[:, :, :].bitcast(I32)).then_inc(s_hand, 1)
                eng.wait_ge(s_free, 3 * NU)
                wait(eng, s_out, 16 * TP * t)
                eng.tensor_copy(resc[:, :, :], resn[:, :, :]).then_inc(s_hand, 1)

            def w1_piece(u):
                n = u
                eng.wait_ge(s_w[n % 4], 16 * (n // 4 + 1))
                scale_of(u, resc[:, n % 4, :], 5 * (u + 1))
                eng.tensor_scalar(resc[:, n % 4, :], resc[:, n % 4, :], rscale[:, u:u + 1].bitcast(F32), None,
                                  ALU.mult).then_inc(s_wsc, 1)
                eng.wait_ge(s_whi, u + 1)
                cols = slice(u * P, (u + 1) * P)
                low(w1l[:, :, cols], psF[u % 2][:, :].rearrange("p (c k) -> p c k", c=NC), w1h[:, :, cols]).then_inc(s_free, 1)

            def w2_max(u):
                n = NU + u
                eng.wait_ge(s_w[n % 4], 16 * (n // 4 + 1))
                eng.tensor_reduce(w2max[:, u:u + 1], resc[:, n % 4, :], AX_X, ALU.max,
                                  apply_absolute_value=True).then_inc(s_free, 1)

            def w2_scale(_):
                eng.wait_ge(s_free, 2 * NU)
                eng.tensor_tensor(w2q[:, :], w2max[:, :], rinv[:, 0:NU].bitcast(F32), ALU.mult).then_inc(s_gc, 1)
                eng.wait_ge(s_gc, 1)
                eng.tensor_reduce(gmax[:, 0:1], w2q[:, :], AX_X, ALU.max).then_inc(s_gc, 1)
                eng.wait_ge(s_gall, 1)
                eng.tensor_scalar(gmax[:, 0:1], gmax[:, 1:2], 1e-30, None, ALU.max).then_inc(s_gc, 1)
                eng.wait_ge(s_gc, 3)
                eng.tensor_scalar(gexp[:, 0:1], gmax[:, 0:1].bitcast(I32), 0x7F800000, None, ALU.bitwise_and).then_inc(s_gc, 1)
                eng.wait_ge(s_gc, 4)
                eng.tensor_scalar(gexp[:, 1:2], gexp[:, 0:1], -1.0, float((254 + W2_EXP) << 23), ALU.mult, ALU.add).then_inc(s_gc, 1)
                eng.tensor_scalar(gexp[:, 2:3], gexp[:, 0:1], float(-(W2_EXP << 23)), None, ALU.add).then_inc(s_gc, 1)
                eng.wait_ge(s_gc, 6)
                eng.tensor_scalar(w2scale[:, :], rinv[:, 0:NU].bitcast(F32), gexp[:, 1:2].bitcast(F32), None, ALU.mult).then_inc(s_gc, 1)
                eng.wait_ge(s_tanh, 1)
                eng.tensor_scalar(ffn_scale[:, :], tanhs[:, 1:2], gexp[:, 2:3].bitcast(F32), None, ALU.mult).then_inc(s_gc, 1)
                eng.wait_ge(s_gc, 8)

            def w2_piece(u):
                n = 2 * NU + u
                s = w2scale[:, u:u + 1]
                eng.wait_ge(s_w[n % 4], 16 * (n // 4 + 1))
                eng.tensor_scalar(w2h[:, u, :], resc[:, n % 4, :], s, None, ALU.mult).then_inc(s_w2hi, 1)
                eng.tensor_scalar(resc[:, n % 4, :], resc[:, n % 4, :], s, None, ALU.mult).then_inc(s_w2hi, 1)

            def units(t, u):
                n = NU * t + u
                eng.wait_ge(s_hhi, n + 1)
                eng.scalar_tensor_tensor(out=hl[:, u, :], in0=psF[u % 2][:, :], scalar=0.0, in1=hh[:, u, :],
                                         op0=ALU.max, op1=ALU.subtract).then_inc(s_h, 1)

            def down(t, j, h):
                if h == 1:
                    eng.wait_ge(s_dps, TP * t + j + 1)
                    eng.wait_ge(s_hand, 4 * t + 4)
                    eng.scalar_tensor_tensor(out=resc[:, j, :], in0=psF[j % 2][:, :], scalar=ffn_scale[:, 0:1],
                                             in1=resc[:, j, :], op0=ALU.mult, op1=ALU.add).then_inc(s_done, 1)

            walk(eng, {"setup": setup, "prep": prep, "proj": proj, "ctx_t": ctx_t, "energy": energy, "shift": shift,
                       "probs": probs, "weigh": weigh, "residual": residual, "x2_t": x2_t, "rank": rank, "mask": mask,
                       "handoff": handoff, "w1": w1_piece, "w2_max": w2_max, "w2_scale": w2_scale, "w2": w2_piece,
                       "units": units, "down": down})

        @block.tensor
        def _(eng):
            mm = eng.matmul

            def bank_free(p, use):
                k = use - RING
                s, per, n = FREE[k % USES]
                wait(eng, s, per * p + n - (per if k < 0 else 0))

            def setup(_):
                eng.wait_ge(s_c1pre, 1)
                for c in range(NC):
                    last = eng.transpose(psE[:, c * P:(c + 1) * P], hraw[:, 5 * P + c * P:5 * P + (c + 1) * P], idf[:, :])
                last.then_inc(s_c1ps, 1)
                eng.wait_ge(s_cast, NCAST)
                eng.wait_ge(s_setup, 1)
                eng.wait_ge(s_const, 4)

            def proj(p, j, b):
                rows = slice(b * C, (b + 1) * C)
                if b == 0:
                    eng.wait_ge(s_hic, p + 1)
                    eng.wait_ge(s_xn, 2 * p + 2)
                    eng.wait_ge(s_loc, 2 * p + 2)
                for i, (wh, wl, vh, vl) in enumerate(((wqh, wql, xh, xl), (wkh, wkl, ch, cl))):
                    n = 2 * b + i
                    bank_free(p, Q0 + n)
                    o = ring[(Q0 + n) % RING][:, :]
                    mm(o, wh[rows, :], vh[rows, :], start=True, stop=False)
                    mm(o, wl[rows, :], vh[rows, :], start=False, stop=False)
                    mm(o, wh[rows, :], vl[rows, :], start=False, stop=True).then_inc(s_qkps, 1)

            def ctx_t(p, j, b):
                bank_free(p, CT0)
                for c in range(NC):
                    cols = slice(c * P, (c + 1) * P)
                    last = eng.transpose(ring[CT0 % RING][:, cols], ct[:, j % 2, cols], idf[:, :])
                last.then_inc(s_ctps, 1)

            def energy(p, j, b):
                eng.wait_ge(s_qk, 4 * p + 2 * b + 2)
                for i in range(NC):
                    bank_free(p, E0 + 4 * b + i)
                    mm(ring[(E0 + 4 * b + i) % RING][:, :], qs[:, b, i * P:(i + 1) * P], ks[:, b, :],
                       start=True, stop=True).then_inc(s_eps, 1)

            def shift(p, j, b):
                use = (S0, S1)[b]
                eng.wait_ge(s_shc, 6 * p + 3 * b + 3)
                bank_free(p, use)
                for c in range(NC):
                    last = eng.transpose(ring[use % RING][:, c * P:(c + 1) * P], shm[:, c, :], idf[:, :])
                last.then_inc(s_shps, 1)

            def probs(p, j, b):
                eng.wait_ge(s_shin, 2 * p + b + 1)
                for i in range(NC):
                    use = (T0, T1)[b] + i
                    bank_free(p, use)
                    mm(ring[use % RING][:, :], ks[:, b, i * P:(i + 1) * P], qs[:, b, :], start=True, stop=True).then_inc(s_tps, 1)

            def weigh(p, j, b):
                eng.wait_ge(s_vt, p + 1)
                wait(eng, s_u, 2 * p + b)
                for i in range(NC):
                    eng.wait_ge(s_thi, 8 * p + 4 * b + i + 1)
                    mm(psU[:, :], vt[:, b, i, :], ph[:, i, :], start=(i == 0), stop=False)
                    eng.wait_ge(s_pl, 8 * p + 4 * b + i + 1)
                    mm(psU[:, :], vt[:, b, i, :], pl[:, i, :], start=False, stop=(i == NC - 1)).then_inc(s_pv, 1)

            def attn_out(p, j, b):
                bank_free(p, O0)
                o = ring[O0 % RING][:, :]
                for b in range(2):
                    eng.wait_ge(s_u, 2 * p + b + 1)
                    mm(o, wvh[:, b, :], uh[:, b, :], start=(b == 0), stop=False)
                    mm(o, wvl[:, b, :], uh[:, b, :], start=False, stop=False)
                    last = mm(o, wvh[:, b, :], ul[:, b, :], start=False, stop=(b == 1))
                last.then_inc(s_ops, 1)

            def x2_t(p, j, b):
                eng.wait_ge(s_x2n, 2 * p + 2)
                wait(eng, s_eq, MC * p)
                for c in range(NC):
                    cols = slice(c * P, (c + 1) * P)
                    last = eng.transpose(psM[:, cols], y[:, cols], idf[:, :])
                last.then_inc(s_x2ps, 1)

            def rank(p, j, b):
                eng.wait_ge(s_x2, p + 1)
                cols = slice(j * P, (j + 1) * P)
                for c in range(NC):
                    mm(psM[:, 0:P], c1h[:, c, :], x2hn[:, c, cols], start=(c == 0), stop=False)
                    mm(psM[:, 0:P], c1l[:, c, :], x2hn[:, c, cols], start=False, stop=False)
                    last = mm(psM[:, 0:P], c1h[:, c, :], x2ln[:, c, cols], start=False, stop=(c == NC - 1))
                last.then_inc(s_rps, 1)

            def mask(p, j, b):
                eng.wait_ge(s_rank, p + 1)
                for c in range(MC):
                    if c > 0:
                        eng.wait_ge(s_eq, MC * p + c)
                    mm(psM[:, 0:MW], ts[:, :], c2s[:, c * MW:(c + 1) * MW], start=True, stop=True).then_inc(s_mps, 1)

            def w1_piece(u):
                eng.wait_ge(s_wsc, u + 1)
                wait(eng, s_free, u - 1)
                for c in range(NC):
                    last = eng.transpose(psF[u % 2][:, c * P:(c + 1) * P], resc[:, u % 4, c * P:(c + 1) * P], idf[:, :])
                last.then_inc(s_wps, 1)

            def turn_mask(t, u):
                if u == 0:
                    eng.wait_ge(s_hand, 4 * t + 3)
                wait(eng, s_eqt, NU * t + u)
                carry_wait(eng)
                for j in range(TP):
                    last = mm(psE[:, j * P:(j + 1) * P], eqc[:, j, u * P:(u + 1) * P], idb[:, :], start=True, stop=True)
                last.then_inc(s_eqps, 1)

            def units(t, u):
                n = NU * t + u
                if u == 0:
                    turn_mask(t, 0)
                if u < 2:
                    wait(eng, s_done, TP * t)
                wait(eng, s_h, NU * t + max(u - 1, 0))
                eng.wait_ge(s_eqt, n + 1)
                o = psF[u % 2][:, :]
                cols = slice(u * P, (u + 1) * P)
                mm(o, tieb[:, :], eqt[:, u % 2, :], start=True, stop=False)
                mm(o, neg_row[:, :], one_row[:, :], start=False, stop=False)
                for c in range(NC):
                    mm(o, w1h[:, c, cols], x2hc[:, c, :], start=False, stop=False)
                    mm(o, w1l[:, c, cols], x2hc[:, c, :], start=False, stop=False)
                    last = mm(o, w1h[:, c, cols], x2lc[:, c, :], start=False, stop=(c == NC - 1))
                last.then_inc(s_hps, 1)
                if u + 1 < NU:
                    turn_mask(t, u + 1)

            def down(t, j, h):
                o = psF[j % 2][:, :]
                if h == 0:
                    eng.wait_ge(s_h, NU * (t + 1))
                    if j >= 2:
                        eng.wait_ge(s_done, TP * t + j - 1)
                cols = slice(j * P, (j + 1) * P)
                for u in range(h * NU // 2, (h + 1) * NU // 2):
                    mm(o, hh[:, u, cols], w2h[:, u, :], start=(u == 0), stop=False)
                    mm(o, hl[:, u, cols], w2h[:, u, :], start=False, stop=False)
                    last = mm(o, hh[:, u, cols], w2l[:, u, :], start=False, stop=(u == NU - 1))
                if h == 1:
                    last.then_inc(s_dps, 1)

            walk(eng, {"setup": setup, "proj": proj, "ctx_t": ctx_t, "energy": energy, "shift": shift, "probs": probs,
                       "weigh": weigh, "attn_out": attn_out, "x2_t": x2_t, "rank": rank, "mask": mask, "w1": w1_piece,
                       "units": units, "down": down})


_DT = {"float32": F32}


def kernel(**inputs):
    import numpy as np
    import concourse.bacc as bacc
    from concourse.bass_utils import run_bass_kernel_spmd as run

    g = {k: np.asarray(v) for k, v in inputs.items()}
    f = np.float32
    zc = np.zeros((C, P - 3 * CH), f)
    wqt, wkt, wvt = g["L0_xattn_Wq"].T, g["L0_xattn_Wk"].T, g["L0_xattn_Wv"].T
    zv = np.zeros((C, C), f)
    z1 = np.zeros((BLK - RANK, N), f)
    z2 = np.zeros((BLK - RANK, INTER), f)
    c1, c2t = g["L0_ffn_c1_w"], g["L0_ffn_c2_w"].T
    zb = np.zeros((P - 3 * CH,), f)
    ones2 = np.concatenate([np.ones((2,), f), np.zeros((P - 3 * CH - 2,), f)])
    u = np.arange(P)
    before = (u[:, None] < u[None, :]) & (u[:, None] // BLK == u[None, :] // BLK)
    tie = (BIG * (np.eye(P) - before)).astype(f)
    arrays = {
        "x": g["x"].reshape(PAIRS, P, N),
        "ctx": g["ctx_4096"].reshape(PAIRS, P, N),
        "w1": g["L0_ffn_w1"].reshape(NU, P, N),
        "w2": g["L0_ffn_w2t"].reshape(NU, P, N),
        "wq": np.concatenate([np.concatenate([wqt, wqt, wqt, zc], 1)] * 2, 0),
        "wk": np.concatenate([np.concatenate([wkt, wkt, wkt, zc], 1)] * 2, 0),
        "wv": np.concatenate([np.concatenate([wvt, zv, zv, wvt], 1)] * 2, 0),
        "bq": np.concatenate([g["L0_xattn_bq"]] * 3 + [zb])[:, None],
        "bk": np.concatenate([g["L0_xattn_bk"]] * 3 + [ones2])[:, None],
        "bv": np.concatenate([g["L0_xattn_bv"]] * 2)[:, None],
        "c1": np.concatenate([c1, z1] * 4, 0),
        "c2": np.concatenate([c2t, z2] * 4, 0),
        "scal": np.tile(np.concatenate([g["g_xattn"], g["g_ffn"], g["L0_xattn_gamma"]])[None, :], (P, 1)),
        "ident": np.eye(P, dtype=f),
        "tie": tie,
    }
    arrays = {k: np.ascontiguousarray(v) for k, v in arrays.items()}
    nc = bacc.Bacc("TRN2", target_bir_lowering=False, num_devices=1, dynamic_dma_scratch_size=8192)
    args = [nc.dram_tensor(f"in_{k}", v.shape, mybir.dt.from_np(v.dtype), kind="ExternalInput").ap()
            for k, v in arrays.items()]
    args.append(nc.dram_tensor("out_0", (PAIRS, P, N), F32, kind="ExternalOutput").ap())
    build(nc, *args)
    r = run(nc, [{f"in_{k}": v for k, v in arrays.items()}], core_ids=[0])
    return r.results[0]["out_0"].reshape(B, C, N)
```

```python
from contextlib import ExitStack

import concourse.bass as bass
from concourse import mybir

F32 = mybir.dt.float32
F32R = mybir.dt.float32r
F16 = mybir.dt.float16
BF16 = mybir.dt.bfloat16
F8 = mybir.dt.float8e4
I32 = mybir.dt.int32
ALU = mybir.AluOpType
ACT = mybir.ActivationFunctionType
AX_X = mybir.AxisListType.X
RMAX = bass.bass_isa.ReduceOp.max

P = 128
B, C, N = 32, 64, 512
CH = C // 2
INTER, BLK, RANK = 1792, 32, 16
PAIRS = B // 2
TP = 2
TILES = PAIRS // TP
SPT = 2 * TP
TOK = TP * P
NU = INTER // P
NC = N // P
MC = 4
MW = INTER // MC
EPS = 1e-5
SH_ROW = 96
BIG = 16384.0
W1_EXP = 3
W2_EXP = 10
RING = 3
SLOTS = 4
SLOT_QK = SPT
STEP = 12
HEAD = 90

BATCH_ITEMS = [(-4.5, "proj", 0), (-4, "proj_high", 0), (-3, "proj_low", 0),
               (-2.5, "proj", 1), (-2, "proj_high", 1), (-1, "proj_low", 1)]
for _i, _b in enumerate((0, 2, 4, 8)):
    BATCH_ITEMS += [(_b + 0.5, "energy", _i), (_b + 1, "energy_max", _i), (_b + 2, "energy_exp", _i)]
BATCH_ITEMS += [(10.3, "ln"), (11.3, "shift"), (12.3, "shift_low"), (13.5, "turn_shift"), (14.1, "put_shift")]
for _i, _b in enumerate((15, 18, 22, 23)):
    BATCH_ITEMS += [(_b + 0.5, "probs", _i), (_b + 1.1, "probs_exp", _i), (_b + 2.2, "probs_low", _i),
                    (_b + 3.6, "weigh", _i)]
BATCH_ITEMS += [(27.2, "u_high"), (28.2, "u_low")]

PAIR_ITEMS = [(-36, "load"), (-22, "stats"), (-18, "stats_sum"), (-17, "power"), (-15, "xn"), (-11, "ctx_high"),
              (-10, "ctx_low"), (-9, "xn_high"), (-8, "xn_low"), (5.5, "ctx_t"), (6.3, "vt_high"), (7.3, "vt_low"),
              (24, "load_residual"), (41.5, "attn_out"), (42.3, "att"), (43, "add_v"), (45, "residual"),
              (46.5, "res_stats"), (47.5, "res_sum"), (48, "res_power"), (49, "norm"), (50.8, "x2_t"), (51.5, "x2_high"),
              (52.5, "x2_low"), (53.8, "rank"), (54.3, "rank_split")]
PAIR_ITEMS += [(55.8 + 2 * _c, "mask", _c) for _c in range(MC)] + [(56.3 + 2 * _c, "pick", _c) for _c in range(MC)]

TILE_ITEMS = [(-6, "give_x2"), (-3, "give_mask"), (2, "give_res", 0), (3, "give_res", 1)]
for _u in range(NU):
    TILE_ITEMS += [(2 * _u - 1.9, "turn", _u), (2 * _u - 0.8, "eqt", _u), (2 * _u, "up", _u, 0), (2 * _u + 1, "up", _u, 1),
                   (2 * _u + 2.05, "relu", _u), (2 * _u + 2.95, "h_low", _u)]
_DOWN = [2 * NU + (_k * (SPT * STEP - 1 - 2 * NU)) // (TP * NU) for _k in range(TP * NU)]
TILE_ITEMS += [(_DOWN[_k], "down", _k // NU, _k % NU) for _k in range(TP * NU)]
TILE_ITEMS += [(_DOWN[NU * (_j + 1) - 1] + 1 - 0.05 * _j, _name, _j) for _j in range(TP) for _name in ("store", "send")]

WEIGHT_ITEMS = []
for _u in range(NU):
    WEIGHT_ITEMS += [(2 * _u + 0.7, "w1_scale", _u), (2 * _u + 1, "w1_mul", _u), (2 * _u + 3.7, "w1_turn", _u),
                     (2 * _u + 4.7, "w1_high", _u), (2 * _u + 5.7, "w1_low", _u), (2 * _u + 5.8, "load_weights", _u + SLOTS),
                     (_u + 32.7, "w2_max", _u), (_u + 32.8, "load_weights", NU + _u + SLOTS),
                     (2.6 * _u + 51, "w2_high", _u), (2.6 * _u + 52, "w2_low", _u),
                     (2.6 * _u + 52.1, "load_weights", 2 * NU + _u + SLOTS)]
WEIGHT_ITEMS += [(4.3, "c2_high"), (6, "c2_low"), (8.2, "more_casts"), (29.7, "c1_scale"), (31, "c1_turn"), (32.2, "c1_high"),
                 (34.1, "c1_low"), (38, "all_made"), (47.5, "w2_largest"), (48, "w2_all"), (50.5, "w2_scale")]

RING_ITEMS = ([(int(b // 1), STEP, n, *r) for b, n, *r in BATCH_ITEMS if n in ("energy", "probs", "proj", "turn_shift")]
              + [(int(b // 1), 2 * STEP, n, *r) for b, n, *r in PAIR_ITEMS if n in ("ctx_t", "attn_out")])
BANK = {tuple(r): b % RING for b, _, *r in RING_ITEMS}


def plan(first, last):
    out = []
    for items, period, count in (([(b + HEAD, *r) for b, *r in TILE_ITEMS], SPT * STEP, TILES), (BATCH_ITEMS, STEP, B), (PAIR_ITEMS, 2 * STEP, PAIRS),
                                 (WEIGHT_ITEMS, 0, 1)):
        for k in range(count):
            out += [(beat + period * k, period, name, k, *part) for beat, name, *part in items
                    if first <= beat + period * k < last]
    return sorted(out, key=lambda item: item[0])


def build(nc, x, ctx, w1, w2, wq, wk, wv, bq, bk, bv, c1, c2, scal, ident, tie, out):
    with ExitStack() as es:
        def sb(name, shape, dt):
            return es.enter_context(nc.sbuf_tensor(name, shape, dt))

        def sem(name):
            return es.enter_context(nc.semaphore(name))

        w1h, w1l = sb("w1h", [P, NC, INTER], F16), sb("w1l", [P, NC, INTER], F16)
        w2h, w2l = sb("w2h", [P, NU, N], F16), sb("w2l", [P, NU, N], F16)
        c1h, c1l = sb("c1h", [P, NC, P], F16), sb("c1l", [P, NC, P], F16)
        c2s = sb("c2s", [P, INTER], F32R)
        wqh, wql = sb("wqh", [P, P], F32R), sb("wql", [P, P], F32R)
        wkh, wkl = sb("wkh", [P, P], F32R), sb("wkl", [P, P], F32R)
        wvh, wvl = sb("wvh", [P, 2, P], F32R), sb("wvl", [P, 2, P], F32R)
        bqc, bkc, bvc = sb("bqc", [P, 1], F32), sb("bkc", [P, 1], F32), sb("bvc", [P, 1], F32)
        sc = sb("sc", [P, 3], F32)
        tanhs = sb("tanhs", [P, 2], F32)
        gbv = sb("gbv", [P, 1], F32)
        ffn_scale = sb("ffn_scale", [P, 1], F32)
        idf = sb("idf", [P, P], F32)
        idb = sb("idb", [P, P], BF16)
        tieb = sb("tieb", [P, P], BF16)
        neg_row, one_row = sb("neg_row", [1, P], BF16), sb("one_row", [1, TOK], BF16)
        half = sb("half", [P, 1], F32)
        rmax, rexp = sb("rmax", [P, NU + 1], F32), sb("rexp", [P, NU + 1], I32)
        rscale, rinv = sb("rscale", [P, NU + 1], I32), sb("rinv", [P, NU + 1], I32)
        w2max, w2q = sb("w2max", [P, NU], F32), sb("w2q", [P, NU], F32)
        gmax = sb("gmax", [P, 2], F32)
        gexp = sb("gexp", [P, 3], I32)
        w2scale = sb("w2scale", [P, NU], F32)
        xt, ct = sb("xt", [P, 2, N], F32), sb("ct", [P, 2, N], F32)
        xn = sb("xn", [P, N], F32)
        xh, xl = sb("xh", [P, N], F32R), sb("xl", [P, N], F32R)
        ch, cl = sb("ch", [P, N], F32R), sb("cl", [P, N], F32R)
        stat, mv, rstd = sb("stat", [P, 2, 6], F32), sb("mv", [P, 2, 2], F32), sb("rstd", [P, 2, 2], F32)
        qs, ks = sb("qs", [P, SLOT_QK, N], F32R), sb("ks", [P, SLOT_QK, N], F32R)
        vt = sb("vt", [P, 2, 2, NC, P], F32R)
        xr, vr = sb("xr", [P, N], F32), sb("vr", [P, N], F32)
        nmax, ssum = sb("nmax", [P, 2, NC], F32), sb("ssum", [P, 2, NC], F32)
        lns, shf = sb("lns", [P, 2, NC], F32), sb("shf", [P, 2, NC], F32)
        shm = sb("shm", [P, NC, P], F32)
        ph, pl = sb("ph", [P, NC, N], F32R), sb("pl", [P, NC, N], F32R)
        pf = sb("pf", [P, 2, N], F32)
        uh, ul = sb("uh", [P, 2, N], F32R), sb("ul", [P, 2, N], F32R)
        att = sb("att", [P, N], F32)
        y = sb("y", [P, N], F32)
        ts = sb("ts", [P, P], F32R)
        bmax = sb("bmax", [P, 2, MW // BLK], F32)
        x2hn, x2ln = sb("x2hn", [P, NC, TOK], F16), sb("x2ln", [P, NC, TOK], F16)
        x2hc, x2lc = sb("x2hc", [P, NC, TOK], F16), sb("x2lc", [P, NC, TOK], F16)
        eqn, eqc = sb("eqn", [P, TP, INTER], F8), sb("eqc", [P, TP, INTER], F8)
        resn, resc = sb("resn", [P, TP, N], F32), sb("resc", [P, TP, N], F32)
        eqt = sb("eqt", [P, 2, TOK], BF16)
        hh, hl = sb("hh", [P, NU, TOK], F16), sb("hl", [P, NU, TOK], F16)

        ring = [es.enter_context(nc.psum_tensor(f"ring{i}", [P, N], F32)) for i in range(RING)]
        psU = es.enter_context(nc.psum_tensor("psU", [P, N], F32))
        psF = [es.enter_context(nc.psum_tensor(f"psF{i}", [P, N], F32)) for i in range(2)]
        psE = es.enter_context(nc.psum_tensor("psE", [P, N], F32))
        psM = es.enter_context(nc.psum_tensor("psM", [P, N], F32))

        s_small, s_x, s_w, s_out = sem("s_small"), [sem("s_x0"), sem("s_x1")], [sem(f"s_w{i}") for i in range(4)], sem("s_out")
        s_const, s_cast, s_tanh, s_c1pre, s_c1ps, s_c1hi, s_more, s_split, s_c2hi, s_w2sc, s_wvhi, s_c2lo = (
            sem(n) for n in ("const", "cast", "tanh", "c1pre", "c1ps", "c1hi", "more", "split", "c2hi", "w2sc", "wvhi", "c2lo"))
        s_rs, s_wsc, s_wps, s_whi, s_wlo, s_free, s_gc, s_gall, s_w2hi, s_w2lo = (
            sem(n) for n in ("rs", "wsc", "wps", "whi", "wlo", "wfree", "gchain", "gall", "w2hi", "w2lo"))
        s_bn, s_pow, s_xn = (sem(n) for n in ("bn", "pow", "xn"))
        s_qkps, s_qkhi, s_qk = sem("qkps"), sem("qkhi"), sem("qk")
        s_ctps, s_cthi, s_vt = sem("ctps"), sem("cthi"), sem("vt")
        s_eps, s_emax, s_eexp = sem("eps"), sem("emax"), sem("eexp")
        s_ln, s_shc, s_shps, s_shin = sem("ln"), sem("shc"), sem("shps"), sem("shin")
        s_tps, s_thi, s_texp, s_pv = sem("tps"), sem("thi"), sem("texp"), sem("pv")
        s_uhi, s_u, s_ops, s_att, s_res = sem("uhi"), sem("u"), sem("ops"), sem("att"), sem("res")
        s_x2ps, s_x2hi, s_x2, s_rps, s_rhi, s_rank = (sem(n) for n in ("x2ps", "x2hi", "x2", "rps", "rhi", "rank"))
        s_mps, s_bmax, s_eq = sem("mps"), sem("bmax"), sem("eq")
        s_gx2, s_gmask, s_gres, s_xr = sem("given_x2"), sem("given_mask"), sem("given_res"), sem("s_xr")
        s_eqps, s_eqt, s_hps, s_hhi, s_h, s_dps, s_done = (
            sem(n) for n in ("eqps", "eqt", "hps", "hhi", "h", "dps", "done"))

        s_passed = {nc.vector.engine: sem("passed_dve"), nc.tensor.engine: sem("passed_pe"),
                    nc.gpsimd.engine: sem("passed_pool")}
        s_chi, s_clo, s_xhi, s_xlo, s_free2, s_pld, s_plp = (sem(n) for n in ("chi", "clo", "xhi", "xlo", "free2", "pld", "plp"))
        s_x2pow, s_rsum, s_rsn, s_x2n = sem("x2pow"), sem("rsum"), sem("rsn"), sem("x2n")
        stage = sb("stage", [P, SLOTS, N], F32)
        hraw = hh.ap().rearrange("p u k -> p (u k)")[:, 0:2 * (5 * P + N)].bitcast(F32)
        c2raw = hl.ap().rearrange("p u k -> p (u k)")[:, 0:2 * INTER].bitcast(F32)
        NSMALL, NMORE = 6, 5
        NCAST, NSPLIT = 4, 5

        block = es.enter_context(nc.Block())

        def wait(eng, s, value):
            if not isinstance(value, int) or value > 0:
                eng.wait_ge(s, value)

        def carry_wait(eng):
            eng.sem_inc(s_passed[eng.engine], 1)

        PF = 2

        def wait_weights(eng, n):
            if n < 2 * NU:
                eng.wait_ge(s_free, n + 1)
            else:
                eng.wait_ge(s_free2, n - 2 * NU + 1)

        here = {"t": 0, "k": 0}

        def pair_of():
            return TP * here["t"] + here["k"] // 2

        def tile_of():
            return here["t"] + here["k"] // TP

        READER = {"energy": (s_eexp, NC), "probs": (s_texp, NC), "proj": (s_qk, 2), "turn_shift": (s_shin, 1),
                  "attn_out": (s_att, 1), "ctx_t": (s_vt, 1)}

        def bank(name, i=0):
            return ring[BANK[(name, i) if (name, i) in BANK else (name,)]][:, :]

        def bank_free(eng, name, i=0):
            own = [(b, period) for b, period, *r in RING_ITEMS if tuple(r) in ((name, i), (name,))][0]
            beat = own[0] + own[1] * here["k"]
            while beat > -2 * STEP:
                beat -= RING
                for b, period, before, *part in RING_ITEMS:
                    k = (beat - b) // period
                    absent = isinstance(here["t"], int) and not 0 <= k < (B if period == STEP else PAIRS)
                    if (beat - b) % period == 0 and not absent:
                        s, per = READER[before]
                        tiles = (SPT if period == STEP else TP) * here["t"]
                        eng.wait_ge(s, per * tiles + (per * k + (part[0] if part else 0) + 1))
                        return

        def walk(eng, steps):
            def go(items, t):
                for _, period, name, k, *part in items:
                    if name not in steps:
                        continue
                    here["t"], here["k"] = t, k
                    if period == STEP:
                        steps[name](SPT * t + k, k % 2, *part)
                    elif period == 2 * STEP:
                        steps[name](TP * t + k, k % 2, *part)
                    elif period:
                        steps[name](t + k, *part)
                    else:
                        steps[name](*part)
            period = SPT * STEP
            loops = TILES - 3
            if "setup" in steps:
                steps["setup"]()
            go(plan(-4 * STEP, HEAD), 0)
            with eng.Fori(0, loops) as t:
                go([(*item[:3], item[3], *item[4:]) for item in plan(HEAD, HEAD + period)], t)
            go(plan(HEAD + loops * period, HEAD + 2 * TILES * period), 0)

        @block.sync
        def _(eng):
            def load(p, slot):
                if p < 2 if isinstance(p, int) else False:
                    return
                eng.wait_ge(s_xn, p - 1)
                eng.wait_ge(s_chi, p - 1)
                eng.wait_ge(s_clo, p - 1)
                eng.wait_ge(s_ctps, p - 1)
                load_now(p, slot)

            def load_now(p, slot):
                eng.dma_start(xt[:, slot, :], x[p]).then_inc(s_x[slot], 16)
                eng.dma_start(ct[:, slot, :], ctx[p]).then_inc(s_x[slot], 16)

            def load_residual(p, slot):
                wait(eng, s_rsum, p)
                wait(eng, s_rsn, p)
                eng.dma_start(xr[:, :], x[p]).then_inc(s_xr, 16)
                eng.dma_start(vr[:, :], ctx[p]).then_inc(s_xr, 16)

            wloads = [(w1, u) for u in range(NU)] + [(w2, u) for u in range(NU)] * 2

            def load_weights(n):
                if n < len(wloads):
                    src, u = wloads[n]
                    if n >= SLOTS:
                        wait_weights(eng, n - SLOTS)
                    eng.dma_start(stage[:, n % SLOTS, :], src[u]).then_inc(s_w[n % SLOTS], 16)

            def setup():
                for dst, src in ((xt[:, 0, :], x[0]), (ct[:, 0, :], ctx[0])):
                    eng.dma_start(dst, src).then_inc(s_x[0], 16)
                for dst, src in ((hraw[:, 0:P], wq), (hraw[:, P:2 * P], wk), (bqc[:, :], bq), (bkc[:, :], bk),
                                 (sc[:, :], scal), (idf[:, :], ident)):
                    eng.dma_start(dst, src).then_inc(s_small, 16)
                for n in range(SLOTS):
                    load_weights(n)
                load_now(1, 1)
                for dst, src in ((c2raw, c2), (hraw[:, 2 * P:4 * P], wv), (hraw[:, 4 * P:5 * P], tie), (bvc[:, :], bv),
                                 (hraw[:, 5 * P:5 * P + N], c1)):
                    eng.dma_start(dst, src).then_inc(s_more, 16)

            def send(t, j):
                eng.wait_ge(s_done, TP * (t + 1) + j + 1)
                eng.dma_start(out[TP * t + j], resc[:, j, :]).then_inc(s_out, 16)

            walk(eng, {"setup": setup, "load": load, "load_residual": load_residual, "load_weights": load_weights, "send": send})
            eng.wait_ge(s_out, 16 * (TP + PAIRS))

        @block.gpsimd
        def _(eng):
            eng.sem_inc(s_done, TP)
            eng.sem_inc(s_out, 16 * TP)
            eng.memset(half[:, :], -0.5).then_inc(s_const, 1)
            eng.memset(neg_row[:, :], -BIG).then_inc(s_const, 1)
            eng.memset(one_row[:, :], 1.0).then_inc(s_const, 1)
            eng.memset(shm[:, :, :], 0.0).then_inc(s_const, 1)
            eng.wait_ge(s_const, 4)

            def power(p, j):
                eng.wait_ge(s_bn, 3 * p + 3)
                wait(eng, s_xn, p)
                eng.tensor_tensor(rstd[:, 0, 1:2], rstd[:, 0, 0:1], half[:, :], ALU.pow).then_inc(s_pow, 1)

            def ctx_low(p, j):
                eng.wait_ge(s_chi, p + 1)
                wait(eng, s_qkps, 4 * p)
                eng.tensor_tensor(cl[:, :], ct[:, j, :], ch[:, :].bitcast(F32), ALU.subtract).then_inc(s_clo, 1)

            def xn_low(p, j):
                eng.wait_ge(s_xhi, p + 1)
                wait(eng, s_qkps, 4 * p)
                eng.tensor_tensor(xl[:, :], xn[:, :], xh[:, :].bitcast(F32), ALU.subtract).then_inc(s_xlo, 1)

            def add_v(q, j):
                eng.wait_ge(s_att, q + 1)
                eng.wait_ge(s_xr, 32 * (q + 1))
                eng.tensor_tensor(att[:, :], att[:, :], vr[:, :], ALU.add).then_inc(s_rsum, 1)

            def res_power(q, j):
                eng.wait_ge(s_res, 3 * q + 3)
                wait(eng, s_x2n, q)
                eng.tensor_tensor(rstd[:, 1, 1:2], rstd[:, 1, 0:1], half[:, :], ALU.pow).then_inc(s_x2pow, 1)

            def w2_all():
                eng.wait_ge(s_gc, 2)
                eng.partition_all_reduce(gmax[:, 1:2], gmax[:, 0:1], P, RMAX).then_inc(s_gall, 1)

            def c2_low():
                eng.wait_ge(s_c2hi, 1)
                eng.wait_ge(s_wsc, 3)
                for n, r in enumerate((32, 96)):
                    rows = slice(r, r + 32)
                    eng.tensor_tensor(c2s[rows, :], c2raw[rows, :], c2s[rows, :].bitcast(F32), ALU.subtract).then_inc(s_c2lo, 1)
                    eng.wait_ge(s_c2lo, n + 1)

            def w1_mul(u):
                sl = stage[:, u % SLOTS, :]
                eng.wait_ge(s_rs, 5 * (u + 1))
                eng.tensor_scalar(sl, sl, rscale[:, u:u + 1].bitcast(F32), None, ALU.mult).then_inc(s_wsc, 1)

            def w2_low(u):
                sl = stage[:, (2 * NU + u) % SLOTS, :]
                eng.wait_ge(s_w2hi, u + 1)
                eng.tensor_scalar(sl, sl, w2scale[:, u:u + 1], None, ALU.mult).then_inc(s_w2sc, 1)
                eng.wait_ge(s_w2sc, u + 1)
                eng.tensor_tensor(w2l[:, u, :], sl, w2h[:, u, :], ALU.subtract).then_inc(s_free2, 1)

            def give_res(t, j):
                eng.wait_ge(s_rsn, TP * t + j + 1)
                eng.wait_ge(s_out, 16 * TP * (t + 1))
                carry_wait(eng)
                eng.tensor_copy(resc[:, j, :], resn[:, j, :]).then_inc(s_gres, 1)

            walk(eng, {"power": power, "ctx_low": ctx_low, "xn_low": xn_low, "add_v": add_v, "res_power": res_power,
                       "w2_all": w2_all, "c2_low": c2_low, "w1_mul": w1_mul, "w2_low": w2_low, "give_res": give_res})

        @block.scalar
        def _(eng):
            act = eng.activation

            def setup():
                eng.wait_ge(s_small, 16 * NSMALL)
                act(tanhs[:, :], sc[:, 0:2], ACT.Tanh).then_inc(s_tanh, 1)
                eng.preload_act_table_set("natural_log_exp_and_others")
                eng.wait_ge(s_cast, NCAST)

            def c2_high():
                eng.wait_ge(s_more, 16 * NMORE)
                act(c2s[:, :], c2raw, ACT.Copy).then_inc(s_c2hi, 1)

            def c1_high():
                eng.wait_ge(s_c1ps, 1)
                act(c1h[:, :, :], psE[:, :].rearrange("p (c r) -> p c r", c=NC), ACT.Copy).then_inc(s_c1hi, 1)

            def all_made():
                eng.wait_ge(s_split, NSPLIT)

            def ctx_high(p, j):
                eng.wait_ge(s_x[j], 16 * (p - j) + 32)
                wait(eng, s_qkps, 4 * p)
                wait(eng, s_clo, p)
                act(ch[:, :], ct[:, j, :], ACT.Copy).then_inc(s_chi, 1)

            def xn_high(p, j):
                eng.wait_ge(s_xn, p + 1)
                wait(eng, s_qkps, 4 * p)
                wait(eng, s_xlo, p)
                act(xh[:, :], xn[:, :], ACT.Copy).then_inc(s_xhi, 1)

            def proj_high(s, b, i):
                dst, bias = ((qs, bqc), (ks, bkc))[i]
                eng.wait_ge(s_qkps, 2 * s + i + 1)
                wait(eng, s_tps, NC * (s - 3))
                act(dst[:, here["k"] % SLOT_QK, :], bank("proj", i), ACT.Identity, bias=bias[:, 0:1]).then_inc(s_qkhi, 1)

            def vt_high(p, j):
                eng.wait_ge(s_ctps, p + 1)
                wait(eng, s_pv, 2 * NC * (p - 1))
                act(vt[:, j, :, :, 0:C], bank("ctx_t").rearrange("p (t b c) -> p b t c", t=NC, b=2), ACT.Copy).then_inc(s_cthi, 1)

            def energy_exp(s, b, i):
                eng.wait_ge(s_emax, NC * s + i + 1)
                if i == 0:
                    wait(eng, s_ln, s - 1)
                o = bank("energy", i)
                act(o, o, ACT.Exp, bias=nmax[:, b, i:i + 1], accum_out=ssum[:, b, i:i + 1]).then_inc(s_eexp, 1)

            def ln(s, b):
                eng.wait_ge(s_eexp, NC * (s + 1))
                wait(eng, s_shc, 3 * (s - 1))
                act(lns[:, b, :], ssum[:, b, :], ACT.Ln).then_inc(s_ln, 1)

            def put_shift(s, b):
                eng.wait_ge(s_shps, s + 1)
                act(qs[SH_ROW:P, here["k"] % SLOT_QK, :], bank("turn_shift")[SH_ROW:P, :], ACT.Copy).then_inc(s_shin, 1)

            def probs_exp(s, b, i):
                o = bank("probs", i)
                eng.wait_ge(s_tps, NC * s + i + 1)
                wait(eng, s_pv, NC * (s - 1) + i + 1)
                act(ph[:, i, :], o, ACT.Exp).then_inc(s_thi, 1)
                wait(eng, s_pld, NC * s + i + 1 - PF)
                act(pf[:, i % PF, :], o, ACT.Exp).then_inc(s_texp, 1)

            def u_high(s, b):
                eng.wait_ge(s_pv, NC * (s + 1))
                wait(eng, s_ops, pair_of())
                act(uh[:, b, :], psU[:, :], ACT.Copy).then_inc(s_uhi, 1)

            def att_(q, j):
                eng.wait_ge(s_ops, q + 1)
                wait(eng, s_rsn, q)
                act(att[:, :], bank("attn_out"), ACT.Identity, bias=gbv[:, 0:1], scale=sc[:, 2:3]).then_inc(s_att, 1)

            def x2_high(q, j):
                eng.wait_ge(s_x2ps, q + 1)
                wait(eng, s_gx2, 2 * tile_of())
                act(x2hn[:, :, j * P:(j + 1) * P], psM[:, :].rearrange("p (c k) -> p c k", c=NC), ACT.Copy).then_inc(s_x2hi, 1)

            def w1_high(u):
                eng.wait_ge(s_wps, u + 1)
                act(w1h[:, :, u * P:(u + 1) * P], psF[u % 2][:, :].rearrange("p (c k) -> p c k", c=NC),
                    ACT.Copy).then_inc(s_whi, 1)

            def w2_high(u):
                n = 2 * NU + u
                sl = stage[:, n % SLOTS, :]
                eng.wait_ge(s_w[n % SLOTS], 16 * (n // SLOTS + 1))
                eng.wait_ge(s_gc, 7)
                act(w2h[:, u, :], sl, ACT.Copy, scale=w2scale[:, u:u + 1]).then_inc(s_w2hi, 1)

            def eqt_copy(t, u):
                eng.wait_ge(s_eqps, NU * t + u + 1)
                if u >= 2:
                    eng.wait_ge(s_hps, NU * t + u - 1)
                act(eqt[:, u % 2, :], psE[:, 0:TOK], ACT.Copy).then_inc(s_eqt, 1)

            def relu(t, u):
                eng.wait_ge(s_hps, NU * t + u + 1)
                act(hh[:, u, :], psF[u % 2][:, 0:TOK], ACT.Relu).then_inc(s_hhi, 1)

            walk(eng, {"setup": setup, "ctx_high": ctx_high, "xn_high": xn_high, "proj_high": proj_high, "vt_high": vt_high,
                       "energy_exp": energy_exp, "ln": ln, "put_shift": put_shift, "probs_exp": probs_exp, "u_high": u_high,
                       "att": att_, "x2_high": x2_high, "w1_high": w1_high, "w2_high": w2_high,
                       "c2_high": c2_high, "c1_high": c1_high, "all_made": all_made, "eqt": eqt_copy, "relu": relu})

        @block.vector
        def _(eng):
            def low(dst, full, high):
                return eng.tensor_tensor(dst, full, high, ALU.subtract)

            def scale_of(col, src, chain):
                eng.tensor_reduce(rmax[:, col:col + 1], src, AX_X, ALU.max, apply_absolute_value=True).then_inc(s_rs, 1)
                eng.wait_ge(s_rs, chain + 1)
                eng.tensor_scalar(rmax[:, col:col + 1], rmax[:, col:col + 1], 1e-30, None, ALU.max).then_inc(s_rs, 1)
                eng.wait_ge(s_rs, chain + 2)
                eng.tensor_scalar(rexp[:, col:col + 1], rmax[:, col:col + 1].bitcast(I32), 0x7F800000, None,
                                  ALU.bitwise_and).then_inc(s_rs, 1)
                eng.wait_ge(s_rs, chain + 3)
                eng.tensor_scalar(rscale[:, col:col + 1], rexp[:, col:col + 1], -1.0, float((254 + W1_EXP) << 23),
                                  ALU.mult, ALU.add).then_inc(s_rs, 1)
                eng.tensor_scalar(rinv[:, col:col + 1], rexp[:, col:col + 1], float(-(W1_EXP << 23)), None,
                                  ALU.add).then_inc(s_rs, 1)
                eng.wait_ge(s_rs, chain + 5)

            def setup():
                eng.wait_ge(s_small, 16 * NSMALL)
                for dst, src in ((wqh, hraw[:, 0:P]), (wkh, hraw[:, P:2 * P])):
                    eng.tensor_copy(dst[:, :], src).then_inc(s_cast, 1)
                eng.wait_ge(s_cast, 2)
                low(wql[:, :], hraw[:, 0:P], wqh[:, :].bitcast(F32)).then_inc(s_cast, 1)
                low(wkl[:, :], hraw[:, P:2 * P], wkh[:, :].bitcast(F32)).then_inc(s_cast, 1)

            def more_casts():
                eng.wait_ge(s_more, 16 * NMORE)
                wvf, wvr = wvh.ap().rearrange("p b k -> p (b k)"), wvl.ap().rearrange("p b k -> p (b k)")
                eng.tensor_copy(wvf, hraw[:, 2 * P:4 * P]).then_inc(s_wvhi, 1)
                eng.tensor_copy(tieb[:, :], hraw[:, 4 * P:5 * P]).then_inc(s_split, 1)
                eng.tensor_copy(idb[:, :], idf[:, :]).then_inc(s_split, 1)
                eng.tensor_tensor(gbv[:, :], bvc[:, :], sc[:, 2:3], ALU.mult).then_inc(s_split, 1)
                eng.wait_ge(s_wvhi, 1)
                low(wvr, hraw[:, 2 * P:4 * P], wvf.bitcast(F32)).then_inc(s_split, 1)

            def c1_scale():
                raw = hraw[:, 5 * P:5 * P + N]
                scale_of(NU, raw, 5 * NU)
                eng.tensor_scalar(raw, raw, rscale[:, NU:NU + 1].bitcast(F32), None, ALU.mult).then_inc(s_c1pre, 1)

            def c1_low():
                eng.wait_ge(s_c1hi, 1)
                low(c1l[:, :, :], psE[:, :].rearrange("p (c r) -> p c r", c=NC), c1h[:, :, :]).then_inc(s_split, 1)

            def stats(p, j):
                eng.wait_ge(s_x[j], 16 * (p - j) + 32)
                eng.bn_stats(stat[:, 0, :], xt[:, j, :]).then_inc(s_bn, 1)

            def stats_sum(p, j):
                wait(eng, s_xn, p)
                eng.wait_ge(s_bn, 3 * p + 1)
                carry_wait(eng)
                eng.bn_aggr(mv[:, 0, :], stat[:, 0, :]).then_inc(s_bn, 1)
                eng.wait_ge(s_bn, 3 * p + 2)
                wait(eng, s_pow, p)
                eng.tensor_scalar(rstd[:, 0, 0:1], mv[:, 0, 1:2], EPS, None, ALU.add).then_inc(s_bn, 1)

            def xn_(p, j):
                eng.wait_ge(s_pow, p + 1)
                wait(eng, s_xlo, p)
                eng.tensor_scalar(xn[:, :], xt[:, j, :], mv[:, 0, 0:1], rstd[:, 0, 1:2], ALU.subtract, ALU.mult).then_inc(s_xn, 1)

            def proj_low(s, b, i):
                dst, bias, row = ((qs, bqc, 64), (ks, bkc, 32))[i]
                rows = slice(row, row + 32)
                eng.wait_ge(s_qkhi, 2 * s + i + 1)
                slot = here["k"] % SLOT_QK
                eng.scalar_tensor_tensor(out=dst[rows, slot, :], in0=bank("proj", i)[rows, :], scalar=bias[rows, 0:1],
                                         in1=dst[rows, slot, :].bitcast(F32), op0=ALU.add, op1=ALU.subtract).then_inc(s_qk, 1)

            def vt_low(p, j):
                eng.wait_ge(s_cthi, p + 1)
                wait(eng, s_pv, 2 * NC * (p - 1))
                low(vt[:, j, :, :, C:P], bank("ctx_t").rearrange("p (t b c) -> p b t c", t=NC, b=2),
                    vt[:, j, :, :, 0:C].bitcast(F32)).then_inc(s_vt, 1)

            def energy_max(s, b, i):
                if i == 0:
                    wait(eng, s_shc, 3 * (s - 1))
                    wait(eng, s_eexp, NC * (s - 1))
                eng.wait_ge(s_eps, NC * s + i + 1)
                eng.tensor_reduce(nmax[:, b, i:i + 1], bank("energy", i), AX_X, ALU.max, negate=True).then_inc(s_emax, 1)

            def shift(s, b):
                eng.wait_ge(s_ln, s + 1)
                eng.wait_ge(s_emax, NC * (s + 1))
                wait(eng, s_shps, s)
                eng.tensor_tensor(shm[:, :, SH_ROW].bitcast(F32R), nmax[:, b, :], lns[:, b, :], ALU.subtract).then_inc(s_shc, 1)
                eng.tensor_tensor(shf[:, b, :], nmax[:, b, :], lns[:, b, :], ALU.subtract).then_inc(s_shc, 1)

            def shift_low(s, b):
                eng.wait_ge(s_shc, 3 * s + 2)
                low(shm[:, :, SH_ROW + 1], shf[:, b, :], shm[:, :, SH_ROW]).then_inc(s_shc, 1)

            def probs_low(s, b, i):
                eng.wait_ge(s_texp, NC * s + i + 1)
                wait(eng, s_pv, NC * (s - 1) + i + 1)
                low(pl[:, i, :], pf[:, i % PF, :], ph[:, i, :].bitcast(F32)).then_inc(s_pld, 1)

            def u_low(s, b):
                eng.wait_ge(s_uhi, s + 1)
                wait(eng, s_ops, pair_of())
                low(ul[:, b, :], psU[:, :], uh[:, b, :].bitcast(F32)).then_inc(s_u, 1)

            def residual(q, j):
                eng.wait_ge(s_rsum, q + 1)
                wait(eng, s_gres, TP * tile_of())
                eng.wait_ge(s_xr, 32 * (q + 1))
                eng.scalar_tensor_tensor(out=resn[:, j, :], in0=att[:, :], scalar=tanhs[:, 0:1], in1=xr[:, :],
                                         op0=ALU.mult, op1=ALU.add).then_inc(s_rsn, 1)

            def res_stats(q, j):
                eng.wait_ge(s_rsn, q + 1)
                eng.bn_stats(stat[:, 1, :], resn[:, j, :]).then_inc(s_res, 1)

            def res_sum(q, j):
                wait(eng, s_x2n, q)
                eng.wait_ge(s_res, 3 * q + 1)
                carry_wait(eng)
                eng.bn_aggr(mv[:, 1, :], stat[:, 1, :]).then_inc(s_res, 1)
                eng.wait_ge(s_res, 3 * q + 2)
                wait(eng, s_x2pow, q)
                eng.tensor_scalar(rstd[:, 1, 0:1], mv[:, 1, 1:2], EPS, None, ALU.add).then_inc(s_res, 1)

            def norm(q, j):
                eng.wait_ge(s_x2pow, q + 1)
                wait(eng, s_x2ps, q)
                eng.tensor_scalar(y[:, :], resn[:, j, :], mv[:, 1, 0:1], rstd[:, 1, 1:2], ALU.subtract,
                                  ALU.mult).then_inc(s_x2n, 1)

            def x2_low(q, j):
                eng.wait_ge(s_x2hi, q + 1)
                cols = slice(j * P, (j + 1) * P)
                low(x2ln[:, :, cols], psM[:, :].rearrange("p (c k) -> p c k", c=NC), x2hn[:, :, cols]).then_inc(s_x2, 1)

            def rank_split(q, j):
                eng.wait_ge(s_rps, q + 1)
                wait(eng, s_mps, MC * q)
                inv = rinv[:, NU:NU + 1].bitcast(F32)
                eng.tensor_scalar(ts[:, :], psM[:, 0:P], inv, None, ALU.mult).then_inc(s_rhi, 1)
                eng.wait_ge(s_rhi, q + 1)
                rows = slice(64, P)
                eng.scalar_tensor_tensor(out=ts[rows, :], in0=psM[rows, 0:P], scalar=inv[rows, :], in1=ts[rows, :].bitcast(F32),
                                         op0=ALU.mult, op1=ALU.subtract).then_inc(s_rank, 1)

            def pick(q, j, c):
                v = psM[:, 0:MW].rearrange("p (n k) -> p n k", k=BLK)
                n = MC * q + c
                eng.wait_ge(s_mps, n + 1)
                wait(eng, s_eq, n - 1)
                bm = bmax[:, c % 2, :]
                eng.tensor_reduce(bm, v, AX_X, ALU.max).then_inc(s_bmax, 1)
                eng.wait_ge(s_bmax, n + 1)
                carry_wait(eng)
                eng.tensor_tensor(eqn[:, j, c * MW:(c + 1) * MW].rearrange("p (n k) -> p n k", k=BLK), v,
                                  bm.unsqueeze(2).broadcast_to([P, MW // BLK, BLK]), ALU.is_equal,
                                  saturate=False).then_inc(s_eq, 1)

            def give_x2(t):
                eng.wait_ge(s_x2, TP * (t + 1))
                eng.wait_ge(s_x2hi, TP * (t + 1))
                wait(eng, s_hps, NU * t)
                eng.tensor_copy(x2hc[:, :, :], x2hn[:, :, :]).then_inc(s_gx2, 1)
                eng.tensor_copy(x2lc[:, :, :], x2ln[:, :, :]).then_inc(s_gx2, 1)

            def give_mask(t):
                eng.wait_ge(s_eq, MC * TP * (t + 1))
                wait(eng, s_eqps, NU * t)
                eng.tensor_copy(eqc[:, :, :].bitcast(I32), eqn[:, :, :].bitcast(I32)).then_inc(s_gmask, 1)

            def w1_scale(u):
                eng.wait_ge(s_w[u % SLOTS], 16 * (u // SLOTS + 1))
                scale_of(u, stage[:, u % SLOTS, :], 5 * u)

            def w1_low(u):
                eng.wait_ge(s_whi, u + 1)
                cols = slice(u * P, (u + 1) * P)
                low(w1l[:, :, cols], psF[u % 2][:, :].rearrange("p (c k) -> p c k", c=NC), w1h[:, :, cols]).then_inc(s_free, 1)

            def w2_max(u):
                n = NU + u
                eng.wait_ge(s_w[n % SLOTS], 16 * (n // SLOTS + 1))
                eng.tensor_reduce(w2max[:, u:u + 1], stage[:, n % SLOTS, :], AX_X, ALU.max,
                                  apply_absolute_value=True).then_inc(s_free, 1)

            def w2_largest():
                eng.wait_ge(s_free, 2 * NU)
                eng.tensor_tensor(w2q[:, :], w2max[:, :], rinv[:, 0:NU].bitcast(F32), ALU.mult).then_inc(s_gc, 1)
                eng.wait_ge(s_gc, 1)
                eng.tensor_reduce(gmax[:, 0:1], w2q[:, :], AX_X, ALU.max).then_inc(s_gc, 1)

            def w2_scale():
                eng.wait_ge(s_gall, 1)
                eng.tensor_scalar(gmax[:, 0:1], gmax[:, 1:2], 1e-30, None, ALU.max).then_inc(s_gc, 1)
                eng.wait_ge(s_gc, 3)
                eng.tensor_scalar(gexp[:, 0:1], gmax[:, 0:1].bitcast(I32), 0x7F800000, None, ALU.bitwise_and).then_inc(s_gc, 1)
                eng.wait_ge(s_gc, 4)
                eng.tensor_scalar(gexp[:, 1:2], gexp[:, 0:1], -1.0, float((254 + W2_EXP) << 23), ALU.mult, ALU.add).then_inc(s_gc, 1)
                eng.tensor_scalar(gexp[:, 2:3], gexp[:, 0:1], float(-(W2_EXP << 23)), None, ALU.add).then_inc(s_gc, 1)
                eng.wait_ge(s_gc, 6)
                eng.tensor_scalar(w2scale[:, :], rinv[:, 0:NU].bitcast(F32), gexp[:, 1:2].bitcast(F32), None, ALU.mult).then_inc(s_gc, 1)
                eng.wait_ge(s_tanh, 1)
                eng.tensor_scalar(ffn_scale[:, :], tanhs[:, 1:2], gexp[:, 2:3].bitcast(F32), None, ALU.mult).then_inc(s_gc, 1)
                eng.wait_ge(s_gc, 8)

            def h_low(t, u):
                eng.wait_ge(s_hhi, NU * t + u + 1)
                eng.scalar_tensor_tensor(out=hl[:, u, :], in0=psF[u % 2][:, 0:TOK], scalar=0.0, in1=hh[:, u, :],
                                         op0=ALU.max, op1=ALU.subtract).then_inc(s_h, 1)

            def store(t, j):
                eng.wait_ge(s_dps, TP * t + j + 1)
                eng.wait_ge(s_gres, TP * t + j + 1)
                eng.scalar_tensor_tensor(out=resc[:, j, :], in0=psF[j % 2][:, :], scalar=ffn_scale[:, 0:1],
                                         in1=resc[:, j, :], op0=ALU.mult, op1=ALU.add).then_inc(s_done, 1)

            walk(eng, {"setup": setup, "more_casts": more_casts, "c1_scale": c1_scale, "c1_low": c1_low, "stats": stats, "stats_sum": stats_sum, "xn": xn_, "proj_low": proj_low, "vt_low": vt_low,
                       "energy_max": energy_max, "shift": shift, "shift_low": shift_low, "probs_low": probs_low, "u_low": u_low,
                       "residual": residual, "res_stats": res_stats, "res_sum": res_sum, "norm": norm, "x2_low": x2_low,
                       "rank_split": rank_split, "pick": pick, "give_x2": give_x2, "give_mask": give_mask,
                       "w1_scale": w1_scale, "w1_low": w1_low, "w2_max": w2_max, "w2_largest": w2_largest, "w2_scale": w2_scale,
                       "h_low": h_low, "store": store})

        @block.tensor
        def _(eng):
            mm = eng.matmul

            def setup():
                eng.wait_ge(s_cast, NCAST)

            def c1_turn():
                eng.wait_ge(s_c1pre, 1)
                for c in range(NC):
                    last = eng.transpose(psE[:, c * P:(c + 1) * P], hraw[:, 5 * P + c * P:5 * P + (c + 1) * P], idf[:, :])
                last.then_inc(s_c1ps, 1)

            def all_made():
                eng.wait_ge(s_split, NSPLIT)
                eng.wait_ge(s_c2lo, 2)
                eng.wait_ge(s_const, 4)

            def proj(s, b, i):
                wh, wl, vh, vl = ((wqh, wql, xh, xl), (wkh, wkl, ch, cl))[i]
                rows = slice(b * C, (b + 1) * C)
                if b == 0:
                    eng.wait_ge((s_xhi, s_chi)[i], pair_of() + 1)
                    eng.wait_ge((s_xlo, s_clo)[i], pair_of() + 1)
                bank_free(eng, "proj", i)
                o = bank("proj", i)
                mm(o, wh[rows, :], vh[rows, :], start=True, stop=False)
                mm(o, wl[rows, :], vh[rows, :], start=False, stop=False)
                mm(o, wh[rows, :], vl[rows, :], start=False, stop=True).then_inc(s_qkps, 1)

            def ctx_t(p, j):
                bank_free(eng, "ctx_t")
                for c in range(NC):
                    cols = slice(c * P, (c + 1) * P)
                    last = eng.transpose(bank("ctx_t")[:, cols], ct[:, j, cols], idf[:, :])
                last.then_inc(s_ctps, 1)

            def energy(s, b, i):
                if i == 0:
                    eng.wait_ge(s_qk, 2 * s + 2)
                bank_free(eng, "energy", i)
                k = here["k"] % SLOT_QK
                mm(bank("energy", i), qs[:, k, i * P:(i + 1) * P], ks[:, k, :], start=True, stop=True).then_inc(s_eps, 1)

            def turn_shift(s, b):
                eng.wait_ge(s_shc, 3 * s + 3)
                bank_free(eng, "turn_shift")
                for c in range(NC):
                    last = eng.transpose(bank("turn_shift")[:, c * P:(c + 1) * P], shm[:, c, :], idf[:, :])
                last.then_inc(s_shps, 1)

            def probs(s, b, i):
                if i == 0:
                    eng.wait_ge(s_shin, s + 1)
                bank_free(eng, "probs", i)
                k = here["k"] % SLOT_QK
                mm(bank("probs", i), ks[:, k, i * P:(i + 1) * P], qs[:, k, :], start=True, stop=True).then_inc(s_tps, 1)

            def weigh(s, b, i):
                if i == 0:
                    eng.wait_ge(s_vt, pair_of() + 1)
                    wait(eng, s_u, s)
                eng.wait_ge(s_thi, NC * s + i + 1)
                pv = vt[:, here["k"] // 2 % 2, b, i, :]
                mm(psU[:, :], pv, ph[:, i, :], start=(i == 0), stop=False)
                eng.wait_ge(s_pld, NC * s + i + 1)
                mm(psU[:, :], pv, pl[:, i, :], start=False, stop=(i == NC - 1)).then_inc(s_pv, 1)

            def attn_out(q, j):
                bank_free(eng, "attn_out")
                o = bank("attn_out")
                eng.wait_ge(s_u, 2 * q + 2)
                for b in range(2):
                    mm(o, wvh[:, b, :], uh[:, b, :], start=(b == 0), stop=False)
                    mm(o, wvl[:, b, :], uh[:, b, :], start=False, stop=False)
                    last = mm(o, wvh[:, b, :], ul[:, b, :], start=False, stop=(b == 1))
                last.then_inc(s_ops, 1)

            def x2_t(q, j):
                eng.wait_ge(s_x2n, q + 1)
                wait(eng, s_eq, MC * q)
                for c in range(NC):
                    cols = slice(c * P, (c + 1) * P)
                    last = eng.transpose(psM[:, cols], y[:, cols], idf[:, :])
                last.then_inc(s_x2ps, 1)

            def rank(q, j):
                eng.wait_ge(s_x2, q + 1)
                cols = slice(j * P, (j + 1) * P)
                for c in range(NC):
                    mm(psM[:, 0:P], c1h[:, c, :], x2hn[:, c, cols], start=(c == 0), stop=False)
                    mm(psM[:, 0:P], c1l[:, c, :], x2hn[:, c, cols], start=False, stop=False)
                    last = mm(psM[:, 0:P], c1h[:, c, :], x2ln[:, c, cols], start=False, stop=(c == NC - 1))
                last.then_inc(s_rps, 1)

            def mask(q, j, c):
                if c == 0:
                    eng.wait_ge(s_rank, q + 1)
                else:
                    eng.wait_ge(s_eq, MC * q + c)
                mm(psM[:, 0:MW], ts[:, :], c2s[:, c * MW:(c + 1) * MW], start=True, stop=True).then_inc(s_mps, 1)

            def w1_turn(u):
                eng.wait_ge(s_wsc, u + 1)
                wait(eng, s_free, u - 1)
                for c in range(NC):
                    last = eng.transpose(psF[u % 2][:, c * P:(c + 1) * P], stage[:, u % SLOTS, c * P:(c + 1) * P], idf[:, :])
                last.then_inc(s_wps, 1)

            def turn(t, u):
                if u == 0:
                    eng.wait_ge(s_gmask, t + 1)
                else:
                    eng.wait_ge(s_eqt, NU * t + u)
                carry_wait(eng)
                for j in range(TP):
                    last = mm(psE[:, j * P:(j + 1) * P], eqc[:, j, u * P:(u + 1) * P], idb[:, :], start=True, stop=True)
                last.then_inc(s_eqps, 1)

            def up(t, u, part):
                o = psF[u % 2][:, 0:TOK]
                cols = slice(u * P, (u + 1) * P)
                if part == 0:
                    if u == 0:
                        eng.wait_ge(s_gx2, 2 * (t + 1))
                        eng.wait_ge(s_done, TP * (t + 1))
                    if u >= 2:
                        eng.wait_ge(s_h, NU * t + u - 1)
                    eng.wait_ge(s_eqt, NU * t + u + 1)
                    mm(o, tieb[:, :], eqt[:, u % 2, :], start=True, stop=False)
                    mm(o, neg_row[:, :], one_row[:, :], start=False, stop=False)
                for c in range(part * NC // 2, (part + 1) * NC // 2):
                    mm(o, w1h[:, c, cols], x2hc[:, c, :], start=False, stop=False)
                    mm(o, w1l[:, c, cols], x2hc[:, c, :], start=False, stop=False)
                    last = mm(o, w1h[:, c, cols], x2lc[:, c, :], start=False, stop=(c == NC - 1))
                if part == 1:
                    last.then_inc(s_hps, 1)

            def down(t, j, u):
                o = psF[j % 2][:, :]
                if u == 0:
                    if j == 0:
                        eng.wait_ge(s_free2, NU)
                    if j == 1:
                        eng.wait_ge(s_h, NU * (t + 1))
                if j == 0:
                    eng.wait_ge(s_h, NU * t + max(u + 1, NU - 1) if u < NU - 1 else NU * (t + 1))
                cols = slice(j * P, (j + 1) * P)
                mm(o, hh[:, u, cols], w2h[:, u, :], start=(u == 0), stop=False)
                mm(o, hl[:, u, cols], w2h[:, u, :], start=False, stop=False)
                last = mm(o, hh[:, u, cols], w2l[:, u, :], start=False, stop=(u == NU - 1))
                if u == NU - 1:
                    last.then_inc(s_dps, 1)

            walk(eng, {"setup": setup, "c1_turn": c1_turn, "all_made": all_made, "proj": proj, "ctx_t": ctx_t, "energy": energy, "turn_shift": turn_shift, "probs": probs,
                       "weigh": weigh, "attn_out": attn_out, "x2_t": x2_t, "rank": rank, "mask": mask, "w1_turn": w1_turn,
                       "turn": turn, "up": up, "down": down})


def kernel(**inputs):
    import numpy as np
    import concourse.bacc as bacc
    from concourse.bass_utils import run_bass_kernel_spmd as run

    g = {k: np.asarray(v) for k, v in inputs.items()}
    f = np.float32
    zc = np.zeros((C, P - 3 * CH), f)
    wqt, wkt, wvt = g["L0_xattn_Wq"].T, g["L0_xattn_Wk"].T, g["L0_xattn_Wv"].T
    zv = np.zeros((C, C), f)
    z1 = np.zeros((BLK - RANK, N), f)
    z2 = np.zeros((BLK - RANK, INTER), f)
    c1, c2t = g["L0_ffn_c1_w"], g["L0_ffn_c2_w"].T
    zb = np.zeros((P - 3 * CH,), f)
    ones2 = np.concatenate([np.ones((2,), f), np.zeros((P - 3 * CH - 2,), f)])
    u = np.arange(P)
    before = (u[:, None] < u[None, :]) & (u[:, None] // BLK == u[None, :] // BLK)
    tie = (BIG * (np.eye(P) - before)).astype(f)
    arrays = {
        "x": g["x"].reshape(PAIRS, P, N),
        "ctx": g["ctx_4096"].reshape(PAIRS, P, N),
        "w1": g["L0_ffn_w1"].reshape(NU, P, N),
        "w2": g["L0_ffn_w2t"].reshape(NU, P, N),
        "wq": np.concatenate([np.concatenate([wqt, wqt, wqt, zc], 1)] * 2, 0),
        "wk": np.concatenate([np.concatenate([wkt, wkt, wkt, zc], 1)] * 2, 0),
        "wv": np.concatenate([np.concatenate([wvt, zv, zv, wvt], 1)] * 2, 0),
        "bq": np.concatenate([g["L0_xattn_bq"]] * 3 + [zb])[:, None],
        "bk": np.concatenate([g["L0_xattn_bk"]] * 3 + [ones2])[:, None],
        "bv": np.concatenate([g["L0_xattn_bv"]] * 2)[:, None],
        "c1": np.concatenate([c1, z1] * 4, 0),
        "c2": np.concatenate([c2t, z2] * 4, 0),
        "scal": np.tile(np.concatenate([g["g_xattn"], g["g_ffn"], g["L0_xattn_gamma"]])[None, :], (P, 1)),
        "ident": np.eye(P, dtype=f),
        "tie": tie,
    }
    arrays = {k: np.ascontiguousarray(v) for k, v in arrays.items()}
    nc = bacc.Bacc("TRN2", target_bir_lowering=False, num_devices=1)
    args = [nc.dram_tensor(f"in_{k}", v.shape, mybir.dt.from_np(v.dtype), kind="ExternalInput").ap()
            for k, v in arrays.items()]
    args.append(nc.dram_tensor("out_0", (PAIRS, P, N), F32, kind="ExternalOutput").ap())
    build(nc, *args)
    r = run(nc, [{f"in_{k}": v for k, v in arrays.items()}], core_ids=[0])
    return r.results[0]["out_0"].reshape(B, C, N)
```

```python
from contextlib import ExitStack

import concourse.bass as bass
from concourse import mybir

F32 = mybir.dt.float32
F32R = mybir.dt.float32r
F16 = mybir.dt.float16
BF16 = mybir.dt.bfloat16
F8 = mybir.dt.float8e4
I32 = mybir.dt.int32
ALU = mybir.AluOpType
ACT = mybir.ActivationFunctionType
AX_X = mybir.AxisListType.X
RMAX = bass.bass_isa.ReduceOp.max

P = 128
B, C, N = 32, 64, 512
CH = C // 2
INTER, BLK, RANK = 1792, 32, 16
PAIRS = B // 2
TP = 2
TILES = PAIRS // TP
SPT = 2 * TP
TOK = TP * P
NU = INTER // P
NC = N // P
MC = 4
MW = INTER // MC
EPS = 1e-5
SH_ROW = 96
BIG = 16384.0
W1_EXP = 3
W2_EXP = 10
RING = 3
SLOTS = 6
SLOT_QK = SPT
STEP = 12
HEAD = 90

BATCH_ITEMS = [(-4.7, "proj", 0), (-3.3, "proj_high", 0), (-2.1, "proj_low", 0),
               (-2.3, "proj", 1), (-1.9, "proj_high", 1), (-0.9, "proj_low", 1)]
for _i, _b in enumerate((0, 2, 4, 8)):
    BATCH_ITEMS += [(_b + 0.1, "energy", _i), (_b + 1, "energy_max", _i), (_b + 2.1, "energy_exp", _i)]
BATCH_ITEMS += [(10.8, "ln"), (11.6, "shift"), (12, "shift_mid"), (12.7, "shift_low"), (13.9, "turn_shift"),
                (14.2, "put_shift")]
for _i, _b in enumerate((15, 18, 22, 23)):
    BATCH_ITEMS += [(_b + 0.4, "probs", _i), (_b + 1.4, "probs_exp", _i), (_b + 2.2, "probs_low", _i),
                    (_b + 3.6, "weigh", _i)]
BATCH_ITEMS += [(27.4, "u_high"), (28.2, "u_low")]

PAIR_ITEMS = [(-34.7, "load"), (-22.1, "stats"), (-20.4, "stats_sum"), (-18.4, "power"), (-16.2, "xn"),
              (-11, "ctx_high"),
              (-9.8, "ctx_low"), (-9.2, "xn_high"), (-8.7, "xn_low"), (5.1, "ctx_t"), (6, "vt_high"), (6.9, "vt_low"),
              (17.5, "load_residual"), (41.1, "attn_out"), (42, "att"), (41.8, "add_v"), (47.5, "residual"),
              (47.6, "res_stats"), (48.2, "res_sum"), (48.8, "res_power"), (49, "norm"), (50.2, "x2_t"),
              (50.8, "x2_high"),
              (51.2, "x2_low"), (53.5, "rank"), (54, "rank_split")]
PAIR_ITEMS += [(55.8 + 2 * _c, "mask", _c) for _c in range(MC)] + [(56.3 + 2 * _c, "pick", _c) for _c in range(MC)]

TILE_ITEMS = [(-11.5, "give_x2"), (-3.3, "give_mask"), (0.5, "give_res", 0), (0.8, "give_res", 1)]
for _u in range(NU):
    TILE_ITEMS += [(2 * _u - 2.1, "turn", _u), (2 * _u - 1.6, "eqt", _u), (2 * _u, "up", _u, 0),
                   (2 * _u + 1.1, "up", _u, 1),
                   (2 * _u + 1.55, "relu", _u), (2 * _u + 2.45, "h_low", _u)]
_DOWN = [2 * NU + (_k * (SPT * STEP - 1 - 2 * NU)) // (TP * NU) for _k in range(TP * NU)]
TILE_ITEMS += [(_DOWN[_k], "down", _k // NU, _k % NU) for _k in range(TP * NU)]
TILE_ITEMS += [(_DOWN[NU * (_j + 1) - 1] + 1 - 0.05 * _j, _name, _j) for _j in range(TP) for _name in ("store", "send")]

WEIGHT_ITEMS = []
for _u in range(NU):
    _b = 5 * (_u // 2) + 1.2 * (_u % 2)
    WEIGHT_ITEMS += [(_b + 1.8, "w1_mul", _u), (_b + 3.5, "w1_turn", _u), (_b + 5, "w1_high", _u),
                     (_b + 5.8, "w1_low", _u),
                     (_b + 2.3, "load_weights", _u + SLOTS), (4 * _u + 56.9, "w2_high", _u),
                     (4.5 * _u + 58, "w2_low", _u),
                     (5.4 * _u + 63.9, "load_weights", 2 * NU + _u + SLOTS)]
for _u in range(0, NU, 2):
    WEIGHT_ITEMS += [(2.4 * _u + 0.4, "w1_scale", _u), (1.2 * _u + 38.5, "w2_max", _u),
                     (1.2 * _u + 36.6, "load_weights", NU + _u + SLOTS),
                     (1.2 * _u + 37.4, "load_weights", NU + _u + SLOTS + 1)]
WEIGHT_ITEMS += [(9.5, "c2_high"), (19.1, "c2_low", 32), (26.3, "c2_low", 96), (6.7, "more_casts"),
                 (34.5, "c1_scale"), (39.2, "c1_turn"),
                 (41.5, "c1_high"), (43.1, "c1_low"), (46, "all_made"), (53.4, "w2_largest"), (57.3, "w2_all"),
                 (56.6, "w2_scale")]

RING_ITEMS = ([(int(b // 1), STEP, n, *r) for b, n, *r in BATCH_ITEMS if n in ("energy", "probs", "proj", "turn_shift")]
              + [(int(b // 1), 2 * STEP, n, *r) for b, n, *r in PAIR_ITEMS if n in ("ctx_t", "attn_out")])
BANK = {tuple(r): b % RING for b, _, *r in RING_ITEMS}


def plan(first, last):
    out = []
    tile_items = [(beat + HEAD, *r) for beat, *r in TILE_ITEMS]
    for items, period, count in ((tile_items, SPT * STEP, TILES), (BATCH_ITEMS, STEP, B), (PAIR_ITEMS, 2 * STEP, PAIRS),
                                 (WEIGHT_ITEMS, 0, 1)):
        for k in range(count):
            out += [(beat + period * k, period, name, k, *part) for beat, name, *part in items
                    if first <= beat + period * k < last]
    return sorted(out, key=lambda item: item[0])


def build(nc, x, ctx, w1, w2, wq, wk, wv, bq, bk, bv, c1, c2, scal, ident, tie, keep, out):
    with ExitStack() as es:
        def sb(name, shape, dt):
            return es.enter_context(nc.sbuf_tensor(name, shape, dt))

        def sem(name):
            return es.enter_context(nc.semaphore(name))

        w1h, w1l = sb("w1h", [P, NC, INTER], F16), sb("w1l", [P, NC, INTER], F16)
        w2h, w2l = sb("w2h", [P, NU, N], F16), sb("w2l", [P, NU, N], F16)
        c1h, c1l = sb("c1h", [P, NC, P], F16), sb("c1l", [P, NC, P], F16)
        c2s = sb("c2s", [P, INTER], F32R)
        wqh, wql = sb("wqh", [P, P], F32R), sb("wql", [P, P], F32R)
        wkh, wkl = sb("wkh", [P, P], F32R), sb("wkl", [P, P], F32R)
        wvh, wvl = sb("wvh", [P, 2, P], F32R), sb("wvl", [P, 2, P], F32R)
        bqc, bkc, bvc = sb("bqc", [P, 1], F32), sb("bkc", [P, 1], F32), sb("bvc", [P, 1], F32)
        sc = sb("sc", [P, 3], F32)
        tanhs = sb("tanhs", [P, 2], F32)
        gbv = sb("gbv", [P, 1], F32)
        ffn_scale = sb("ffn_scale", [P, 1], F32)
        idf = sb("idf", [P, P], F32)
        idb = sb("idb", [P, P], BF16)
        tieb = sb("tieb", [P, P], BF16)
        kept = sb("kept", [P, 2], F32)
        half = sb("half", [P, 1], F32)
        rmax, rexp = sb("rmax", [P, NU + 1], F32), sb("rexp", [P, NU + 1], I32)
        rscale, rinv = sb("rscale", [P, NU + 1], I32), sb("rinv", [P, NU + 1], I32)
        w2max, w2q = sb("w2max", [P, NU], F32), sb("w2q", [P, NU], F32)
        gmax = sb("gmax", [P, 2], F32)
        gexp = sb("gexp", [P, 3], I32)
        w2scale = sb("w2scale", [P, NU], F32)
        xt, ct = sb("xt", [P, 2, N], F32), sb("ct", [P, 2, N], F32)
        xn = sb("xn", [P, N], F32)
        xs, cs = sb("xs", [P, 2, N], F32R), sb("cs", [P, 2, N], F32R)
        stat, mv, rstd = sb("stat", [P, 2, 6], F32), sb("mv", [P, 2, 2], F32), sb("rstd", [P, 2, 2], F32)
        qs, ks = sb("qs", [P, SLOT_QK, N], F32R), sb("ks", [P, SLOT_QK, N], F32R)
        vt = sb("vt", [P, 2, 2, NC, P], F32R)
        xr, vr = sb("xr", [P, N], F32), sb("vr", [P, N], F32)
        nmax, ssum = sb("nmax", [P, 2, NC], F32), sb("ssum", [P, 2, NC], F32)
        lns, shf = sb("lns", [P, 2, NC], F32), sb("shf", [P, 2, NC], F32)
        shm, shr = sb("shm", [P, NC, P], BF16), sb("shr", [P, 2, NC], F32)
        ph, pl = sb("ph", [P, NC, N], F32R), sb("pl", [P, NC, N], F32R)
        pf = sb("pf", [P, 2, N], F32)
        uh, ul = sb("uh", [P, 2, N], F32R), sb("ul", [P, 2, N], F32R)
        att = sb("att", [P, N], F32)
        y = sb("y", [P, N], F32)
        ts = sb("ts", [P, P], F32R)
        bmax = sb("bmax", [P, 2, MW // BLK], F32)
        x2hn, x2ln = sb("x2hn", [P, NC, TOK], F16), sb("x2ln", [P, NC, TOK], F16)
        x2hc, x2lc = sb("x2hc", [P, NC, TOK], F16), sb("x2lc", [P, NC, TOK], F16)
        eqn, eqc = sb("eqn", [P, TP, INTER], F8), sb("eqc", [P, TP, INTER], F8)
        resn, resc = sb("resn", [P, TP, N], F32), sb("resc", [P, TP, N], F32)
        eqt = sb("eqt", [P, 2, TOK], BF16)
        hh, hl = sb("hh", [P, NU, TOK], F16), sb("hl", [P, NU, TOK], F16)

        ring = [es.enter_context(nc.psum_tensor(f"ring{i}", [P, N], F32)) for i in range(RING)]
        psU = es.enter_context(nc.psum_tensor("psU", [P, N], F32))
        psF = [es.enter_context(nc.psum_tensor(f"psF{i}", [P, N], F32)) for i in range(2)]
        psE = es.enter_context(nc.psum_tensor("psE", [P, N], F32))
        psM = es.enter_context(nc.psum_tensor("psM", [P, N], F32))

        s_small, s_more, s_x = sem("small"), sem("more"), [sem("x0"), sem("x1")]
        s_w, s_xr, s_out = [sem(f"w{i}") for i in range(SLOTS)], sem("xr"), sem("out")
        s_const, s_cast, s_tanh, s_c1pre, s_c1ps, s_c1hi, s_split, s_wvhi, s_c2hi, s_c2lo = (
            sem(n) for n in ("const", "cast", "tanh", "c1pre", "c1ps", "c1hi", "split", "wvhi", "c2hi", "c2lo"))
        s_rs, s_wsc, s_muls, s_wps, s_whi, s_free = (sem(n) for n in ("rs", "wsc", "muls", "wps", "whi", "wfree"))
        s_gc, s_gall, s_w2hi, s_w2sc, s_free2, s_free3 = (
            sem(n) for n in ("gchain", "gall", "w2hi", "w2sc", "free2", "free3"))
        s_bn, s_pow, s_xn = (sem(n) for n in ("bn", "pow", "xn"))
        s_xhi, s_xlo, s_chi, s_clo = (sem(n) for n in ("xhi", "xlo", "chi", "clo"))
        s_qkps, s_qkhi, s_qk, s_ctps, s_cthi, s_vt = (sem(n) for n in ("qkps", "qkhi", "qk", "ctps", "cthi", "vt"))
        s_eps, s_emax, s_eexp = (sem(n) for n in ("eps", "emax", "eexp"))
        s_ln, s_shc, s_shps, s_shin = (sem(n) for n in ("ln", "shc", "shps", "shin"))
        s_tps, s_thi, s_texp, s_pv = (sem(n) for n in ("tps", "thi", "texp", "pv"))
        s_pl = [sem(f"pl{i}") for i in range(NC)]
        s_uhi, s_u, s_ops, s_att, s_rsum, s_rsn, s_res = (sem(n) for n in ("uhi", "u", "ops", "att", "rsum", "rsn", "res"))
        s_x2pow, s_x2n, s_x2ps, s_x2hi, s_x2 = (sem(n) for n in ("x2pow", "x2n", "x2ps", "x2hi", "x2"))
        s_rps, s_rhi, s_rank = (sem(n) for n in ("rps", "rhi", "rank"))
        s_mps, s_bmax, s_eq = (sem(n) for n in ("mps", "bmax", "eq"))
        s_gx2, s_gmask, s_gres = (sem(n) for n in ("given_x2", "given_mask", "given_res"))
        s_eqps, s_eqt, s_hps, s_hhi, s_h, s_dps, s_done = (
            sem(n) for n in ("eqps", "eqt", "hps", "hhi", "h", "dps", "done"))
        s_passed = {nc.vector.engine: sem("passed_dve"), nc.tensor.engine: sem("passed_pe"),
                    nc.gpsimd.engine: sem("passed_pool")}
        stage = sb("stage", [P, SLOTS, N], F32)
        hraw = hh.ap().rearrange("p u k -> p (u k)")[:, 0:2 * (5 * P + N)].bitcast(F32)
        c2raw = hl.ap().rearrange("p u k -> p (u k)")[:, 0:2 * INTER].bitcast(F32)
        NSMALL, NMORE = 7, 5
        NCAST, NSPLIT = 5, 4

        block = es.enter_context(nc.Block())

        def wait(eng, s, value):
            if not isinstance(value, int) or value > 0:
                eng.wait_ge(s, value)

        def carry_wait(eng):
            eng.sem_inc(s_passed[eng.engine], 1)

        PF = 2
        POOL_LOW = 2

        def wait_weights(eng, n):
            u = n - 2 * NU
            if u < 0:
                eng.wait_ge(s_free, n + 1)
            else:
                eng.wait_ge(s_free3 if u % 2 else s_free2, u // 2 + 1)

        def halves(b):
            return slice(b * C, (b + 1) * C), slice((1 - b) * C, (2 - b) * C)

        here = {"t": 0, "k": 0}

        def pair_of():
            return TP * here["t"] + here["k"] // 2

        def tile_of():
            return here["t"] + here["k"] // TP

        READER = {"energy": (s_eexp, NC), "probs": (s_texp, NC), "proj": (s_qk, 2), "turn_shift": (s_shin, 1),
                  "attn_out": (s_att, 1), "ctx_t": (s_vt, 1)}

        def bank(name, i=0):
            return ring[BANK[(name, i) if (name, i) in BANK else (name,)]][:, :]

        def bank_free(eng, name, i=0):
            own = [(b, period) for b, period, *r in RING_ITEMS if tuple(r) in ((name, i), (name,))][0]
            beat = own[0] + own[1] * here["k"]
            while beat > -2 * STEP:
                beat -= RING
                for b, period, before, *part in RING_ITEMS:
                    k = (beat - b) // period
                    absent = isinstance(here["t"], int) and not 0 <= k < (B if period == STEP else PAIRS)
                    if (beat - b) % period == 0 and not absent:
                        s, per = READER[before]
                        tiles = (SPT if period == STEP else TP) * here["t"]
                        eng.wait_ge(s, per * tiles + (per * k + (part[0] if part else 0) + 1))
                        return

        def walk(eng, steps):
            def go(items, t):
                for _, period, name, k, *part in items:
                    if name not in steps:
                        continue
                    here["t"], here["k"] = t, k
                    if period == STEP:
                        steps[name](SPT * t + k, k % 2, *part)
                    elif period == 2 * STEP:
                        steps[name](TP * t + k, k % 2, *part)
                    elif period:
                        steps[name](t + k, *part)
                    else:
                        steps[name](*part)
            period = SPT * STEP
            first = HEAD + 2 * NU
            loops = TILES - 4
            if "setup" in steps:
                steps["setup"]()
            go([item for item in plan(-4 * STEP, first) if item[2:4] not in (("load", 0), ("load", 1))], 0)
            with eng.Fori(0, loops) as t:
                go(plan(first, first + period), t)
            go(plan(first + loops * period, first + TILES * period), 0)

        @block.sync
        def _(eng):
            def load(p, slot):
                eng.wait_ge(s_xn, p - 1)
                eng.wait_ge(s_ctps, p - 1)
                load_now(p, slot)

            def load_now(p, slot):
                eng.dma_start(xt[:, slot, :], x[p]).then_inc(s_x[slot], 16)
                eng.dma_start(ct[:, slot, :], ctx[p]).then_inc(s_x[slot], 16)

            def load_residual(p, slot):
                wait(eng, s_rsum, p)
                wait(eng, s_rsn, p)
                eng.dma_start(xr[:, :], x[p]).then_inc(s_xr, 16)
                eng.dma_start(vr[:, :], ctx[p]).then_inc(s_xr, 16)

            wloads = [(w1, u) for u in range(NU)] + [(w2, u) for u in range(NU)] * 2

            def load_weights(n):
                if n < len(wloads):
                    src, u = wloads[n]
                    if n >= SLOTS:
                        wait_weights(eng, n - SLOTS)
                    eng.dma_start(stage[:, n % SLOTS, :], src[u]).then_inc(s_w[n % SLOTS], 16)

            def setup():
                for dst, src in ((xt[:, 0, :], x[0]), (ct[:, 0, :], ctx[0])):
                    eng.dma_start(dst, src).then_inc(s_x[0], 16)
                for dst, src in ((hraw[:, 0:P], wq), (hraw[:, P:2 * P], wk), (bqc[:, :], bq), (bkc[:, :], bk),
                                 (sc[:, :], scal), (kept[:, :], keep), (idf[:, :], ident)):
                    eng.dma_start(dst, src).then_inc(s_small, 16)
                for n in range(SLOTS):
                    load_weights(n)
                load_now(1, 1)
                for dst, src in ((c2raw, c2), (hraw[:, 2 * P:4 * P], wv), (hraw[:, 4 * P:5 * P], tie), (bvc[:, :], bv),
                                 (hraw[:, 5 * P:5 * P + N], c1)):
                    eng.dma_start(dst, src).then_inc(s_more, 16)

            def send(t, j):
                eng.wait_ge(s_done, TP * t + j + 1)
                eng.dma_start(out[TP * t + j], resc[:, j, :]).then_inc(s_out, 16)

            walk(eng, {"setup": setup, "load": load, "load_residual": load_residual, "load_weights": load_weights,
                       "send": send})
            eng.wait_ge(s_out, 16 * PAIRS)

        @block.gpsimd
        def _(eng):
            eng.memset(half[:, :], -0.5).then_inc(s_const, 1)
            eng.memset(shm[:, :, :], 0.0).then_inc(s_const, 1)
            eng.wait_ge(s_const, 2)

            def power(p, j):
                eng.wait_ge(s_bn, 3 * p + 3)
                wait(eng, s_xn, p)
                eng.tensor_tensor(rstd[:, 0, 1:2], rstd[:, 0, 0:1], half[:, :], ALU.pow).then_inc(s_pow, 1)
                eng.wait_ge(s_pow, p + 1)

            def ctx_low(p, j):
                wait(eng, s_qkps, 4 * p)
                for b in range(2):
                    hi, lo = halves(b)
                    eng.wait_ge(s_chi, 2 * p + b + 1)
                    eng.tensor_tensor(cs[lo, b, :], ct[hi, j, :], cs[hi, b, :].bitcast(F32), ALU.subtract).then_inc(s_clo, 1)
                    eng.wait_ge(s_clo, 2 * p + b + 1)

            def xn_low(p, j):
                wait(eng, s_qkps, 4 * p)
                for b in range(2):
                    hi, lo = halves(b)
                    eng.wait_ge(s_xhi, 2 * p + b + 1)
                    eng.tensor_tensor(xs[lo, b, :], xn[hi, :], xs[hi, b, :].bitcast(F32), ALU.subtract).then_inc(s_xlo, 1)
                    eng.wait_ge(s_xlo, 2 * p + b + 1)

            def probs_low(s, b, i):
                if i == POOL_LOW:
                    eng.wait_ge(s_texp, NC * s + i + 1)
                    wait(eng, s_pv, NC * (s - 1) + i + 1)
                    eng.tensor_tensor(pl[:, i, :], pf[:, i % PF, :], ph[:, i, :].bitcast(F32), ALU.subtract).then_inc(s_pl[i], 1)
                    eng.wait_ge(s_pl[i], s + 1)

            def add_v(q, j):
                eng.wait_ge(s_att, q + 1)
                eng.wait_ge(s_xr, 32 * (q + 1))
                eng.tensor_tensor(att[:, :], att[:, :], vr[:, :], ALU.add).then_inc(s_rsum, 1)
                eng.wait_ge(s_rsum, q + 1)

            def res_power(q, j):
                eng.wait_ge(s_res, 3 * q + 3)
                wait(eng, s_x2n, q)
                eng.tensor_tensor(rstd[:, 1, 1:2], rstd[:, 1, 0:1], half[:, :], ALU.pow).then_inc(s_x2pow, 1)
                eng.wait_ge(s_x2pow, q + 1)

            def c2_low(r):
                eng.wait_ge(s_c2hi, 1)
                rows = slice(r, r + 32)
                eng.tensor_tensor(c2s[rows, :], c2raw[rows, :], c2s[rows, :].bitcast(F32), ALU.subtract).then_inc(s_c2lo, 1)
                eng.wait_ge(s_c2lo, (32, 96).index(r) + 1)

            def w1_mul(u):
                if u % 2:
                    sl = stage[:, u % SLOTS, :]
                    eng.wait_ge(s_rs, 5 * (u // 2 + 1))
                    eng.tensor_scalar(sl, sl, rscale[:, u:u + 1].bitcast(F32), None, ALU.mult).then_inc(s_muls, 1)
                    eng.wait_ge(s_muls, u // 2 + 1)

            def w2_all():
                eng.wait_ge(s_gc, 2)
                eng.partition_all_reduce(gmax[:, 1:2], gmax[:, 0:1], P, RMAX).then_inc(s_gall, 1)
                eng.wait_ge(s_gall, 1)

            def w2_low(u):
                if u % 2:
                    sl = stage[:, (2 * NU + u) % SLOTS, :]
                    eng.wait_ge(s_w2hi, u + 1)
                    eng.tensor_scalar(sl, sl, w2scale[:, u:u + 1], None, ALU.mult).then_inc(s_w2sc, 1)
                    eng.wait_ge(s_w2sc, u // 2 + 1)
                    eng.tensor_tensor(w2l[:, u, :], sl, w2h[:, u, :], ALU.subtract).then_inc(s_free3, 1)
                    eng.wait_ge(s_free3, u // 2 + 1)

            def give_res(t, j):
                eng.wait_ge(s_rsn, TP * t + j + 1)
                wait(eng, s_out, 16 * TP * t)
                carry_wait(eng)
                eng.tensor_copy(resc[:, j, :], resn[:, j, :]).then_inc(s_gres, 1)
                eng.wait_ge(s_gres, TP * t + j + 1)

            walk(eng, {"power": power, "probs_low": probs_low, "c2_low": c2_low, "w1_mul": w1_mul, "ctx_low": ctx_low,
                       "xn_low": xn_low, "add_v": add_v, "res_power": res_power, "w2_all": w2_all, "w2_low": w2_low,
                       "give_res": give_res})

        @block.scalar
        def _(eng):
            act = eng.activation

            def setup():
                eng.wait_ge(s_small, 16 * NSMALL)
                act(tanhs[:, :], sc[:, 0:2], ACT.Tanh).then_inc(s_tanh, 1)
                eng.preload_act_table_set("natural_log_exp_and_others")
                eng.wait_ge(s_cast, NCAST)

            def c2_high():
                eng.wait_ge(s_more, 16 * NMORE)
                act(c2s[:, :], c2raw, ACT.Copy).then_inc(s_c2hi, 1)

            def c1_high():
                eng.wait_ge(s_c1ps, 1)
                act(c1h[:, :, :], psE[:, :].rearrange("p (c r) -> p c r", c=NC), ACT.Copy).then_inc(s_c1hi, 1)

            def all_made():
                eng.wait_ge(s_split, NSPLIT)

            def ctx_high(p, j):
                eng.wait_ge(s_x[j], 16 * (p - j) + 32)
                wait(eng, s_qkps, 4 * p)
                for b in range(2):
                    hi, _ = halves(b)
                    act(cs[hi, b, :], ct[hi, j, :], ACT.Copy).then_inc(s_chi, 1)

            def xn_high(p, j):
                eng.wait_ge(s_xn, p + 1)
                wait(eng, s_qkps, 4 * p)
                for b in range(2):
                    hi, _ = halves(b)
                    act(xs[hi, b, :], xn[hi, :], ACT.Copy).then_inc(s_xhi, 1)

            def proj_high(s, b, i):
                dst, bias = ((qs, bqc), (ks, bkc))[i]
                eng.wait_ge(s_qkps, 2 * s + i + 1)
                wait(eng, s_tps, NC * (s - 3))
                act(dst[:, here["k"] % SLOT_QK, :], bank("proj", i), ACT.Identity, bias=bias[:, 0:1]).then_inc(s_qkhi, 1)

            def vt_high(p, j):
                eng.wait_ge(s_ctps, p + 1)
                wait(eng, s_pv, 2 * NC * (p - 1))
                act(vt[:, j, :, :, 0:C], bank("ctx_t").rearrange("p (t b c) -> p b t c", t=NC, b=2), ACT.Copy).then_inc(s_cthi, 1)

            def energy_exp(s, b, i):
                eng.wait_ge(s_emax, NC * s + i + 1)
                if i == 0:
                    wait(eng, s_ln, s - 1)
                o = bank("energy", i)
                act(o, o, ACT.Exp, bias=nmax[:, b, i:i + 1], accum_out=ssum[:, b, i:i + 1]).then_inc(s_eexp, 1)

            def ln(s, b):
                eng.wait_ge(s_eexp, NC * (s + 1))
                wait(eng, s_shc, 5 * (s - 1))
                act(lns[:, b, :], ssum[:, b, :], ACT.Ln).then_inc(s_ln, 1)

            def put_shift(s, b):
                eng.wait_ge(s_shps, s + 1)
                act(qs[SH_ROW:P, here["k"] % SLOT_QK, :], bank("turn_shift")[SH_ROW:P, :], ACT.Copy).then_inc(s_shin, 1)

            def probs_exp(s, b, i):
                o = bank("probs", i)
                eng.wait_ge(s_tps, NC * s + i + 1)
                wait(eng, s_pv, NC * (s - 1) + i + 1)
                act(ph[:, i, :], o, ACT.Exp).then_inc(s_thi, 1)
                wait(eng, s_pl[(i - PF) % NC], s + (i >= PF))
                act(pf[:, i % PF, :], o, ACT.Exp).then_inc(s_texp, 1)

            def u_high(s, b):
                eng.wait_ge(s_pv, NC * (s + 1))
                wait(eng, s_ops, pair_of())
                act(uh[:, b, :], psU[:, :], ACT.Copy).then_inc(s_uhi, 1)

            def att_(q, j):
                eng.wait_ge(s_ops, q + 1)
                wait(eng, s_rsn, q)
                act(att[:, :], bank("attn_out"), ACT.Identity, bias=gbv[:, 0:1], scale=sc[:, 2:3]).then_inc(s_att, 1)

            def x2_high(q, j):
                eng.wait_ge(s_x2ps, q + 1)
                wait(eng, s_gx2, 2 * tile_of())
                act(x2hn[:, :, j * P:(j + 1) * P], psM[:, :].rearrange("p (c k) -> p c k", c=NC), ACT.Copy).then_inc(s_x2hi, 1)

            def w1_mul(u):
                if u % 2 == 0:
                    sl = stage[:, u % SLOTS, :]
                    eng.wait_ge(s_rs, 5 * (u // 2 + 1))
                    act(sl, sl, ACT.Copy, scale=rscale[:, u:u + 1].bitcast(F32)).then_inc(s_wsc, 1)

            def w1_high(u):
                eng.wait_ge(s_wps, u + 1)
                act(w1h[:, :, u * P:(u + 1) * P], psF[u % 2][:, :].rearrange("p (c k) -> p c k", c=NC),
                    ACT.Copy).then_inc(s_whi, 1)

            def w2_high(u):
                n = 2 * NU + u
                sl = stage[:, n % SLOTS, :]
                eng.wait_ge(s_w[n % SLOTS], 16 * (n // SLOTS + 1))
                eng.wait_ge(s_gc, 7)
                act(w2h[:, u, :], sl, ACT.Copy, scale=w2scale[:, u:u + 1]).then_inc(s_w2hi, 1)

            def eqt_copy(t, u):
                eng.wait_ge(s_eqps, NU * t + u + 1)
                if u >= 2:
                    eng.wait_ge(s_hps, NU * t + u - 1)
                act(eqt[:, u % 2, :], psE[:, 0:TOK], ACT.Identity, bias=kept[:, 1:2], scale=kept[:, 0:1]).then_inc(s_eqt, 1)

            def relu(t, u):
                eng.wait_ge(s_hps, NU * t + u + 1)
                act(hh[:, u, :], psF[u % 2][:, 0:TOK], ACT.Relu).then_inc(s_hhi, 1)

            walk(eng, {"setup": setup, "ctx_high": ctx_high, "xn_high": xn_high, "proj_high": proj_high,
                       "vt_high": vt_high, "energy_exp": energy_exp, "ln": ln, "put_shift": put_shift,
                       "probs_exp": probs_exp, "u_high": u_high, "att": att_, "x2_high": x2_high, "w1_mul": w1_mul,
                       "w1_high": w1_high, "w2_high": w2_high, "c2_high": c2_high, "c1_high": c1_high,
                       "all_made": all_made, "eqt": eqt_copy, "relu": relu})

        @block.vector
        def _(eng):
            def low(dst, full, high):
                return eng.tensor_tensor(dst, full, high, ALU.subtract)

            def scale_of(col, src, chain, width=1):
                eng.tensor_reduce(rmax[:, col:col + width], src, AX_X, ALU.max, apply_absolute_value=True).then_inc(s_rs, 1)
                eng.wait_ge(s_rs, chain + 1)
                eng.tensor_scalar(rmax[:, col:col + width], rmax[:, col:col + width], 1e-30, None, ALU.max).then_inc(s_rs, 1)
                eng.wait_ge(s_rs, chain + 2)
                eng.tensor_scalar(rexp[:, col:col + width], rmax[:, col:col + width].bitcast(I32), 0x7F800000, None,
                                  ALU.bitwise_and).then_inc(s_rs, 1)
                eng.wait_ge(s_rs, chain + 3)
                eng.tensor_scalar(rscale[:, col:col + width], rexp[:, col:col + width], -1.0, float((254 + W1_EXP) << 23),
                                  ALU.mult, ALU.add).then_inc(s_rs, 1)
                eng.tensor_scalar(rinv[:, col:col + width], rexp[:, col:col + width], float(-(W1_EXP << 23)), None,
                                  ALU.add).then_inc(s_rs, 1)
                eng.wait_ge(s_rs, chain + 5)

            def setup():
                eng.wait_ge(s_small, 16 * NSMALL)
                for dst, src in ((wqh, hraw[:, 0:P]), (wkh, hraw[:, P:2 * P])):
                    eng.tensor_copy(dst[:, :], src).then_inc(s_cast, 1)
                eng.tensor_copy(idb[:, :], idf[:, :]).then_inc(s_cast, 1)
                eng.wait_ge(s_cast, 3)
                low(wql[:, :], hraw[:, 0:P], wqh[:, :].bitcast(F32)).then_inc(s_cast, 1)
                low(wkl[:, :], hraw[:, P:2 * P], wkh[:, :].bitcast(F32)).then_inc(s_cast, 1)

            def more_casts():
                eng.wait_ge(s_more, 16 * NMORE)
                wvf, wvr = wvh.ap().rearrange("p b k -> p (b k)"), wvl.ap().rearrange("p b k -> p (b k)")
                eng.tensor_copy(wvf, hraw[:, 2 * P:4 * P]).then_inc(s_wvhi, 1)
                eng.tensor_copy(tieb[:, :], hraw[:, 4 * P:5 * P]).then_inc(s_split, 1)
                eng.tensor_tensor(gbv[:, :], bvc[:, :], sc[:, 2:3], ALU.mult).then_inc(s_split, 1)
                eng.wait_ge(s_wvhi, 1)
                low(wvr, hraw[:, 2 * P:4 * P], wvf.bitcast(F32)).then_inc(s_split, 1)

            def c1_scale():
                raw = hraw[:, 5 * P:5 * P + N]
                scale_of(NU, raw, 5 * NU // 2)
                eng.tensor_scalar(raw, raw, rscale[:, NU:NU + 1].bitcast(F32), None, ALU.mult).then_inc(s_c1pre, 1)

            def c1_low():
                eng.wait_ge(s_c1hi, 1)
                low(c1l[:, :, :], psE[:, :].rearrange("p (c r) -> p c r", c=NC), c1h[:, :, :]).then_inc(s_split, 1)

            def stats(p, j):
                eng.wait_ge(s_x[j], 16 * (p - j) + 32)
                eng.bn_stats(stat[:, 0, :], xt[:, j, :]).then_inc(s_bn, 1)

            def stats_sum(p, j):
                wait(eng, s_xn, p)
                eng.wait_ge(s_bn, 3 * p + 1)
                carry_wait(eng)
                eng.bn_aggr(mv[:, 0, :], stat[:, 0, :]).then_inc(s_bn, 1)
                eng.wait_ge(s_bn, 3 * p + 2)
                wait(eng, s_pow, p)
                eng.tensor_scalar(rstd[:, 0, 0:1], mv[:, 0, 1:2], EPS, None, ALU.add).then_inc(s_bn, 1)

            def xn_(p, j):
                eng.wait_ge(s_pow, p + 1)
                wait(eng, s_xlo, 2 * p)
                eng.tensor_scalar(xn[:, :], xt[:, j, :], mv[:, 0, 0:1], rstd[:, 0, 1:2], ALU.subtract, ALU.mult).then_inc(s_xn, 1)

            def proj_low(s, b, i):
                dst, bias, row = ((qs, bqc, 64), (ks, bkc, 32))[i]
                rows = slice(row, row + 32)
                eng.wait_ge(s_qkhi, 2 * s + i + 1)
                slot = here["k"] % SLOT_QK
                eng.scalar_tensor_tensor(out=dst[rows, slot, :], in0=bank("proj", i)[rows, :], scalar=bias[rows, 0:1],
                                         in1=dst[rows, slot, :].bitcast(F32), op0=ALU.add, op1=ALU.subtract).then_inc(s_qk, 1)

            def vt_low(p, j):
                eng.wait_ge(s_cthi, p + 1)
                wait(eng, s_pv, 2 * NC * (p - 1))
                low(vt[:, j, :, :, C:P], bank("ctx_t").rearrange("p (t b c) -> p b t c", t=NC, b=2),
                    vt[:, j, :, :, 0:C].bitcast(F32)).then_inc(s_vt, 1)

            def energy_max(s, b, i):
                if i == 0:
                    wait(eng, s_shc, 5 * (s - 1))
                    wait(eng, s_eexp, NC * (s - 1))
                eng.wait_ge(s_eps, NC * s + i + 1)
                eng.tensor_reduce(nmax[:, b, i:i + 1], bank("energy", i), AX_X, ALU.max, negate=True).then_inc(s_emax, 1)

            def shift(s, b):
                eng.wait_ge(s_ln, s + 1)
                eng.wait_ge(s_emax, NC * (s + 1))
                wait(eng, s_shps, s)
                eng.tensor_tensor(shm[:, :, SH_ROW], nmax[:, b, :], lns[:, b, :], ALU.subtract).then_inc(s_shc, 1)
                eng.tensor_tensor(shf[:, b, :], nmax[:, b, :], lns[:, b, :], ALU.subtract).then_inc(s_shc, 1)

            def shift_mid(s, b):
                eng.wait_ge(s_shc, 5 * s + 2)
                low(shm[:, :, SH_ROW + 1], shf[:, b, :], shm[:, :, SH_ROW]).then_inc(s_shc, 1)
                low(shr[:, b, :], shf[:, b, :], shm[:, :, SH_ROW]).then_inc(s_shc, 1)

            def shift_low(s, b):
                eng.wait_ge(s_shc, 5 * s + 4)
                low(shm[:, :, SH_ROW + 2], shr[:, b, :], shm[:, :, SH_ROW + 1]).then_inc(s_shc, 1)

            def probs_low(s, b, i):
                if i == POOL_LOW:
                    return
                eng.wait_ge(s_texp, NC * s + i + 1)
                wait(eng, s_pv, NC * (s - 1) + i + 1)
                low(pl[:, i, :], pf[:, i % PF, :], ph[:, i, :].bitcast(F32)).then_inc(s_pl[i], 1)

            def u_low(s, b):
                eng.wait_ge(s_uhi, s + 1)
                wait(eng, s_ops, pair_of())
                low(ul[:, b, :], psU[:, :], uh[:, b, :].bitcast(F32)).then_inc(s_u, 1)

            def residual(q, j):
                eng.wait_ge(s_rsum, q + 1)
                wait(eng, s_gres, TP * tile_of())
                eng.wait_ge(s_xr, 32 * (q + 1))
                eng.scalar_tensor_tensor(out=resn[:, j, :], in0=att[:, :], scalar=tanhs[:, 0:1], in1=xr[:, :],
                                         op0=ALU.mult, op1=ALU.add).then_inc(s_rsn, 1)

            def res_stats(q, j):
                eng.wait_ge(s_rsn, q + 1)
                eng.bn_stats(stat[:, 1, :], resn[:, j, :]).then_inc(s_res, 1)

            def res_sum(q, j):
                wait(eng, s_x2n, q)
                eng.wait_ge(s_res, 3 * q + 1)
                carry_wait(eng)
                eng.bn_aggr(mv[:, 1, :], stat[:, 1, :]).then_inc(s_res, 1)
                eng.wait_ge(s_res, 3 * q + 2)
                wait(eng, s_x2pow, q)
                eng.tensor_scalar(rstd[:, 1, 0:1], mv[:, 1, 1:2], EPS, None, ALU.add).then_inc(s_res, 1)

            def norm(q, j):
                eng.wait_ge(s_x2pow, q + 1)
                wait(eng, s_x2ps, q)
                eng.tensor_scalar(y[:, :], resn[:, j, :], mv[:, 1, 0:1], rstd[:, 1, 1:2], ALU.subtract,
                                  ALU.mult).then_inc(s_x2n, 1)

            def x2_low(q, j):
                eng.wait_ge(s_x2hi, q + 1)
                cols = slice(j * P, (j + 1) * P)
                low(x2ln[:, :, cols], psM[:, :].rearrange("p (c k) -> p c k", c=NC), x2hn[:, :, cols]).then_inc(s_x2, 1)

            def rank_split(q, j):
                eng.wait_ge(s_rps, q + 1)
                wait(eng, s_mps, MC * q)
                inv = rinv[:, NU:NU + 1].bitcast(F32)
                eng.tensor_scalar(ts[:, :], psM[:, 0:P], inv, None, ALU.mult).then_inc(s_rhi, 1)
                eng.wait_ge(s_rhi, q + 1)
                rows = slice(64, P)
                eng.scalar_tensor_tensor(out=ts[rows, :], in0=psM[rows, 0:P], scalar=inv[rows, :], in1=ts[rows, :].bitcast(F32),
                                         op0=ALU.mult, op1=ALU.subtract).then_inc(s_rank, 1)

            def pick(q, j, c):
                v = psM[:, 0:MW].rearrange("p (n k) -> p n k", k=BLK)
                n = MC * q + c
                eng.wait_ge(s_mps, n + 1)
                wait(eng, s_eq, n - 1)
                bm = bmax[:, c % 2, :]
                eng.tensor_reduce(bm, v, AX_X, ALU.max).then_inc(s_bmax, 1)
                eng.wait_ge(s_bmax, n + 1)
                carry_wait(eng)
                eng.tensor_tensor(eqn[:, j, c * MW:(c + 1) * MW].rearrange("p (n k) -> p n k", k=BLK), v,
                                  bm.unsqueeze(2).broadcast_to([P, MW // BLK, BLK]), ALU.is_equal,
                                  saturate=False).then_inc(s_eq, 1)

            def give_x2(t):
                eng.wait_ge(s_x2, TP * (t + 1))
                eng.wait_ge(s_x2hi, TP * (t + 1))
                wait(eng, s_hps, NU * t)
                eng.tensor_copy(x2hc[:, :, :], x2hn[:, :, :]).then_inc(s_gx2, 1)
                eng.tensor_copy(x2lc[:, :, :], x2ln[:, :, :]).then_inc(s_gx2, 1)

            def give_mask(t):
                eng.wait_ge(s_eq, MC * TP * (t + 1))
                wait(eng, s_eqps, NU * t)
                eng.tensor_copy(eqc[:, :, :].bitcast(I32), eqn[:, :, :].bitcast(I32)).then_inc(s_gmask, 1)

            def w1_scale(u):
                for v in (u, u + 1):
                    eng.wait_ge(s_w[v % SLOTS], 16 * (v // SLOTS + 1))
                scale_of(u, stage[:, u % SLOTS:u % SLOTS + 2, :], 5 * (u // 2), width=2)

            def w1_low(u):
                eng.wait_ge(s_whi, u + 1)
                cols = slice(u * P, (u + 1) * P)
                low(w1l[:, :, cols], psF[u % 2][:, :].rearrange("p (c k) -> p c k", c=NC), w1h[:, :, cols]).then_inc(s_free, 1)

            def w2_max(u):
                n = NU + u
                for v in (n, n + 1):
                    eng.wait_ge(s_w[v % SLOTS], 16 * (v // SLOTS + 1))
                eng.tensor_reduce(w2max[:, u:u + 2], stage[:, n % SLOTS:n % SLOTS + 2, :], AX_X, ALU.max,
                                  apply_absolute_value=True).then_inc(s_free, 2)

            def w2_largest():
                eng.wait_ge(s_free, 2 * NU)
                eng.tensor_tensor(w2q[:, :], w2max[:, :], rinv[:, 0:NU].bitcast(F32), ALU.mult).then_inc(s_gc, 1)
                eng.wait_ge(s_gc, 1)
                eng.tensor_reduce(gmax[:, 0:1], w2q[:, :], AX_X, ALU.max).then_inc(s_gc, 1)

            def w2_scale():
                eng.wait_ge(s_gall, 1)
                eng.tensor_scalar(gmax[:, 0:1], gmax[:, 1:2], 1e-30, None, ALU.max).then_inc(s_gc, 1)
                eng.wait_ge(s_gc, 3)
                eng.tensor_scalar(gexp[:, 0:1], gmax[:, 0:1].bitcast(I32), 0x7F800000, None, ALU.bitwise_and).then_inc(s_gc, 1)
                eng.wait_ge(s_gc, 4)
                eng.tensor_scalar(gexp[:, 1:2], gexp[:, 0:1], -1.0, float((254 + W2_EXP) << 23), ALU.mult, ALU.add).then_inc(s_gc, 1)
                eng.tensor_scalar(gexp[:, 2:3], gexp[:, 0:1], float(-(W2_EXP << 23)), None, ALU.add).then_inc(s_gc, 1)
                eng.wait_ge(s_gc, 6)
                eng.tensor_scalar(w2scale[:, :], rinv[:, 0:NU].bitcast(F32), gexp[:, 1:2].bitcast(F32), None, ALU.mult).then_inc(s_gc, 1)
                eng.wait_ge(s_tanh, 1)
                eng.tensor_scalar(ffn_scale[:, :], tanhs[:, 1:2], gexp[:, 2:3].bitcast(F32), None, ALU.mult).then_inc(s_gc, 1)
                eng.wait_ge(s_gc, 8)

            def w2_low(u):
                if u % 2 == 0:
                    eng.wait_ge(s_w2hi, u + 1)
                    eng.scalar_tensor_tensor(out=w2l[:, u, :], in0=stage[:, (2 * NU + u) % SLOTS, :],
                                             scalar=w2scale[:, u:u + 1], in1=w2h[:, u, :], op0=ALU.mult,
                                             op1=ALU.subtract).then_inc(s_free2, 1)

            def h_low(t, u):
                eng.wait_ge(s_hhi, NU * t + u + 1)
                eng.scalar_tensor_tensor(out=hl[:, u, :], in0=psF[u % 2][:, 0:TOK], scalar=0.0, in1=hh[:, u, :],
                                         op0=ALU.max, op1=ALU.subtract).then_inc(s_h, 1)

            def store(t, j):
                eng.wait_ge(s_dps, TP * t + j + 1)
                eng.wait_ge(s_gres, TP * t + j + 1)
                eng.scalar_tensor_tensor(out=resc[:, j, :], in0=psF[j % 2][:, :], scalar=ffn_scale[:, 0:1],
                                         in1=resc[:, j, :], op0=ALU.mult, op1=ALU.add).then_inc(s_done, 1)

            walk(eng, {"setup": setup, "more_casts": more_casts, "w2_low": w2_low, "c1_scale": c1_scale,
                       "c1_low": c1_low, "stats": stats, "stats_sum": stats_sum, "xn": xn_, "proj_low": proj_low,
                       "vt_low": vt_low, "energy_max": energy_max, "shift": shift, "shift_mid": shift_mid,
                       "shift_low": shift_low, "probs_low": probs_low, "u_low": u_low, "residual": residual,
                       "res_stats": res_stats, "res_sum": res_sum, "norm": norm, "x2_low": x2_low,
                       "rank_split": rank_split, "pick": pick, "give_x2": give_x2, "give_mask": give_mask,
                       "w1_scale": w1_scale, "w1_low": w1_low, "w2_max": w2_max, "w2_largest": w2_largest,
                       "w2_scale": w2_scale, "h_low": h_low, "store": store})

        @block.tensor
        def _(eng):
            mm = eng.matmul

            def setup():
                eng.wait_ge(s_cast, NCAST)

            def c1_turn():
                eng.wait_ge(s_c1pre, 1)
                for c in range(NC):
                    last = eng.transpose(psE[:, c * P:(c + 1) * P], hraw[:, 5 * P + c * P:5 * P + (c + 1) * P], idf[:, :])
                last.then_inc(s_c1ps, 1)

            def all_made():
                eng.wait_ge(s_split, NSPLIT)
                eng.wait_ge(s_c2lo, 2)
                eng.wait_ge(s_const, 2)

            def proj(s, b, i):
                wh, wl, v = ((wqh, wql, xs), (wkh, wkl, cs))[i]
                hi, _ = halves(b)
                eng.wait_ge((s_xhi, s_chi)[i], 2 * pair_of() + b + 1)
                eng.wait_ge((s_xlo, s_clo)[i], 2 * pair_of() + b + 1)
                bank_free(eng, "proj", i)
                o = bank("proj", i)
                mm(o, wh[:, :], v[:, b, :], start=True, stop=False)
                mm(o, wl[hi, :], v[hi, b, :], start=False, stop=True).then_inc(s_qkps, 1)

            def ctx_t(p, j):
                bank_free(eng, "ctx_t")
                for c in range(NC):
                    cols = slice(c * P, (c + 1) * P)
                    last = eng.transpose(bank("ctx_t")[:, cols], ct[:, j, cols], idf[:, :])
                last.then_inc(s_ctps, 1)

            def energy(s, b, i):
                if i == 0:
                    eng.wait_ge(s_qk, 2 * s + 2)
                bank_free(eng, "energy", i)
                k = here["k"] % SLOT_QK
                mm(bank("energy", i), qs[:, k, i * P:(i + 1) * P], ks[:, k, :], start=True, stop=True).then_inc(s_eps, 1)

            def turn_shift(s, b):
                eng.wait_ge(s_shc, 5 * s + 5)
                bank_free(eng, "turn_shift")
                for c in range(NC):
                    last = mm(bank("turn_shift")[:, c * P:(c + 1) * P], shm[:, c, :], idb[:, :], start=True, stop=True)
                last.then_inc(s_shps, 1)

            def probs(s, b, i):
                if i == 0:
                    eng.wait_ge(s_shin, s + 1)
                bank_free(eng, "probs", i)
                k = here["k"] % SLOT_QK
                mm(bank("probs", i), ks[:, k, i * P:(i + 1) * P], qs[:, k, :], start=True, stop=True).then_inc(s_tps, 1)

            def weigh(s, b, i):
                if i == 0:
                    eng.wait_ge(s_vt, pair_of() + 1)
                    wait(eng, s_u, s)
                eng.wait_ge(s_thi, NC * s + i + 1)
                pv = vt[:, here["k"] // 2 % 2, b, i, :]
                mm(psU[:, :], pv, ph[:, i, :], start=(i == 0), stop=False)
                eng.wait_ge(s_pl[i], s + 1)
                mm(psU[:, :], pv, pl[:, i, :], start=False, stop=(i == NC - 1)).then_inc(s_pv, 1)

            def attn_out(q, j):
                bank_free(eng, "attn_out")
                o = bank("attn_out")
                eng.wait_ge(s_u, 2 * q + 2)
                for b in range(2):
                    mm(o, wvh[:, b, :], uh[:, b, :], start=(b == 0), stop=False)
                    mm(o, wvl[:, b, :], uh[:, b, :], start=False, stop=False)
                    last = mm(o, wvh[:, b, :], ul[:, b, :], start=False, stop=(b == 1))
                last.then_inc(s_ops, 1)

            def x2_t(q, j):
                eng.wait_ge(s_x2n, q + 1)
                wait(eng, s_eq, MC * q)
                for c in range(NC):
                    cols = slice(c * P, (c + 1) * P)
                    last = eng.transpose(psM[:, cols], y[:, cols], idf[:, :])
                last.then_inc(s_x2ps, 1)

            def rank(q, j):
                eng.wait_ge(s_x2, q + 1)
                cols = slice(j * P, (j + 1) * P)
                for c in range(NC):
                    mm(psM[:, 0:P], c1h[:, c, :], x2hn[:, c, cols], start=(c == 0), stop=False)
                    mm(psM[:, 0:P], c1l[:, c, :], x2hn[:, c, cols], start=False, stop=False)
                    last = mm(psM[:, 0:P], c1h[:, c, :], x2ln[:, c, cols], start=False, stop=(c == NC - 1))
                last.then_inc(s_rps, 1)

            def mask(q, j, c):
                if c == 0:
                    eng.wait_ge(s_rank, q + 1)
                else:
                    eng.wait_ge(s_eq, MC * q + c)
                mm(psM[:, 0:MW], ts[:, :], c2s[:, c * MW:(c + 1) * MW], start=True, stop=True).then_inc(s_mps, 1)

            def w1_turn(u):
                eng.wait_ge(s_muls if u % 2 else s_wsc, u // 2 + 1)
                wait(eng, s_free, u - 1)
                for c in range(NC):
                    last = eng.transpose(psF[u % 2][:, c * P:(c + 1) * P], stage[:, u % SLOTS, c * P:(c + 1) * P], idf[:, :])
                last.then_inc(s_wps, 1)

            def turn(t, u):
                if u == 0:
                    eng.wait_ge(s_gmask, t + 1)
                else:
                    eng.wait_ge(s_eqt, NU * t + u)
                carry_wait(eng)
                for j in range(TP):
                    last = mm(psE[:, j * P:(j + 1) * P], eqc[:, j, u * P:(u + 1) * P], idb[:, :], start=True, stop=True)
                last.then_inc(s_eqps, 1)

            def up(t, u, part):
                o = psF[u % 2][:, 0:TOK]
                cols = slice(u * P, (u + 1) * P)
                if part == 0:
                    if u == 0:
                        eng.wait_ge(s_gx2, 2 * (t + 1))
                        wait(eng, s_done, TP * t)
                    if u >= 2:
                        eng.wait_ge(s_h, NU * t + u - 1)
                    eng.wait_ge(s_eqt, NU * t + u + 1)
                    mm(o, tieb[:, :], eqt[:, u % 2, :], start=True, stop=False)
                for c in range(part * NC // 2, (part + 1) * NC // 2):
                    mm(o, w1h[:, c, cols], x2hc[:, c, :], start=False, stop=False)
                    mm(o, w1l[:, c, cols], x2hc[:, c, :], start=False, stop=False)
                    last = mm(o, w1h[:, c, cols], x2lc[:, c, :], start=False, stop=(c == NC - 1))
                if part == 1:
                    last.then_inc(s_hps, 1)

            def down(t, j, u):
                o = psF[j % 2][:, :]
                if u == 0:
                    if j == 0:
                        eng.wait_ge(s_free2, NU // 2)
                        eng.wait_ge(s_free3, NU // 2)
                    if j == 1:
                        eng.wait_ge(s_h, NU * (t + 1))
                if j == 0:
                    eng.wait_ge(s_h, NU * t + max(u + 1, NU - 1) if u < NU - 1 else NU * (t + 1))
                cols = slice(j * P, (j + 1) * P)
                mm(o, hh[:, u, cols], w2h[:, u, :], start=(u == 0), stop=False)
                mm(o, hl[:, u, cols], w2h[:, u, :], start=False, stop=False)
                last = mm(o, hh[:, u, cols], w2l[:, u, :], start=False, stop=(u == NU - 1))
                if u == NU - 1:
                    last.then_inc(s_dps, 1)

            walk(eng, {"setup": setup, "c1_turn": c1_turn, "all_made": all_made, "proj": proj, "ctx_t": ctx_t,
                       "energy": energy, "turn_shift": turn_shift, "probs": probs, "weigh": weigh,
                       "attn_out": attn_out, "x2_t": x2_t, "rank": rank, "mask": mask, "w1_turn": w1_turn,
                       "turn": turn, "up": up, "down": down})


def kernel(**inputs):
    import numpy as np
    import concourse.bacc as bacc
    from concourse.bass_utils import run_bass_kernel_spmd as run

    g = {k: np.asarray(v) for k, v in inputs.items()}
    f = np.float32
    zc = np.zeros((C, P - 3 * CH), f)
    wqt, wkt, wvt = g["L0_xattn_Wq"].T, g["L0_xattn_Wk"].T, g["L0_xattn_Wv"].T
    zv = np.zeros((C, C), f)
    z1 = np.zeros((BLK - RANK, N), f)
    z2 = np.zeros((BLK - RANK, INTER), f)
    c1, c2t = g["L0_ffn_c1_w"], g["L0_ffn_c2_w"].T
    zb = np.zeros((P - 3 * CH,), f)
    ones3 = np.concatenate([np.ones((3,), f), np.zeros((P - 3 * CH - 3,), f)])
    u = np.arange(P)
    before = (u[:, None] < u[None, :]) & (u[:, None] // BLK == u[None, :] // BLK)
    last = u % BLK == BLK - 1
    tie = (BIG * (np.eye(P) * ~last - before - (last[:, None] & before.T))).astype(f)
    arrays = {
        "x": g["x"].reshape(PAIRS, P, N),
        "ctx": g["ctx_4096"].reshape(PAIRS, P, N),
        "w1": g["L0_ffn_w1"].reshape(NU, P, N),
        "w2": g["L0_ffn_w2t"].reshape(NU, P, N),
        "wq": np.concatenate([np.concatenate([wqt, wqt, wqt, zc], 1)] * 2, 0),
        "wk": np.concatenate([np.concatenate([wkt, wkt, wkt, zc], 1)] * 2, 0),
        "wv": np.concatenate([np.concatenate([wvt, zv, zv, wvt], 1)] * 2, 0),
        "bq": np.concatenate([g["L0_xattn_bq"]] * 3 + [zb])[:, None],
        "bk": np.concatenate([g["L0_xattn_bk"]] * 3 + [ones3])[:, None],
        "bv": np.concatenate([g["L0_xattn_bv"]] * 2)[:, None],
        "c1": np.concatenate([c1, z1] * 4, 0),
        "c2": np.concatenate([c2t, z2] * 4, 0),
        "scal": np.tile(np.concatenate([g["g_xattn"], g["g_ffn"], g["L0_xattn_gamma"]])[None, :], (P, 1)),
        "ident": np.eye(P, dtype=f),
        "tie": tie,
        "keep": np.stack([~last, last], 1).astype(f),
    }
    arrays = {k: np.ascontiguousarray(v) for k, v in arrays.items()}
    nc = bacc.Bacc("TRN2", target_bir_lowering=False, num_devices=1)
    args = [nc.dram_tensor(f"in_{k}", v.shape, mybir.dt.from_np(v.dtype), kind="ExternalInput").ap()
            for k, v in arrays.items()]
    args.append(nc.dram_tensor("out_0", (PAIRS, P, N), F32, kind="ExternalOutput").ap())
    build(nc, *args)
    r = run(nc, [{f"in_{k}": v for k, v in arrays.items()}], core_ids=[0])
    return r.results[0]["out_0"].reshape(B, C, N)
```
